# Optimizing a Trainium2 kernel written in Bass

```python
import numpy as np
import jax
import jax.numpy as jnp

def _softmax(x, axis=-1):
    return jax.nn.softmax(x, axis=axis)

def _gelu(x):
    return jax.nn.gelu(x, approximate=True)

def _silu(x):
    return jax.nn.silu(x)

def _sigmoid(x):
    return jax.nn.sigmoid(x)

def _layernorm(x, axis=-1, eps=1e-05):
    m = jnp.mean(x, axis=axis, keepdims=True)
    v = jnp.var(x, axis=axis, keepdims=True)
    return (x - m) / jnp.sqrt(v + eps)

def _scatter_add(tgt, idx, src, axis=0):
    return tgt.at[idx].add(src)

def _segment_sum(src, seg, n):
    return jax.ops.segment_sum(src, seg, n)
kernel_name = 'mk_gnn_resnorm_d4_gnn_r8_1e282f'

def setup_inputs(seed: int=0):
    np.random.seed(seed)
    _w = jnp.asarray

    def _rec_inputs():
        import jax
        import jax.numpy as jnp
        _gk = jax.random.key(seed)
        x = -0.000202 + 1 * jax.random.normal(jax.random.fold_in(_gk, 1), (6250, 128), jnp.float32)
        _s = jax.random.randint(jax.random.fold_in(_gk, 2), (50000,), 0, 6250, jnp.int32)
        _d = jax.random.randint(jax.random.fold_in(_gk, 3), (50000,), 0, 6250, jnp.int32)
        _loop = jnp.arange(6250, dtype=jnp.int32)
        src = jnp.concatenate([_s, _d, _loop])
        dst = jnp.concatenate([_d, _s, _loop])
        _o = jnp.argsort(dst, stable=True)
        src = src[_o]
        dst = dst[_o]
        edge_attr_128 = -6.47781e-05 + 0.999943 * jax.random.normal(jax.random.fold_in(_gk, 12), (106250, 128), jnp.float32)
        return (x, src, dst, edge_attr_128)
    x, src, dst, edge_attr_128 = _rec_inputs()

    def _L0_gnn_setup():
        import jax, jax.numpy as jnp
        import numpy as np
        N_NODES = 6250
        N_EDGES = 75000
        D = 128
        key = jax.random.key(seed)
        k1, k2, k3, k4, k5 = jax.random.split(key, 5)
        x = jax.random.normal(k1, (N_NODES, D), dtype=jnp.float32)
        W = jax.random.normal(k2, (D, 2 * D), dtype=jnp.float32) * (1.0 / np.sqrt(2 * D))
        b = jax.random.normal(k3, (D,), dtype=jnp.float32) * 0.01
        src = jax.random.randint(k4, (N_EDGES,), 0, N_NODES, dtype=jnp.int32)
        dst = jax.random.randint(k5, (N_EDGES,), 0, N_NODES, dtype=jnp.int32)
        return {'x': x, 'W': W, 'b': b, 'src': src, 'dst': dst}
    _L0_gnn_all = _L0_gnn_setup()
    _L0_gnn_in = {k: v for k, v in _L0_gnn_all.items() if k in ('W', 'b')}
    del _L0_gnn_all

    def _L1_gnn_setup():
        import jax, jax.numpy as jnp
        import numpy as np
        N_NODES = 12500
        N_EDGES = 200000
        EMBED = 128
        LN_EPS = 1e-05
        NEG_SLOPE = 0.01

        def _calc_messages(H, E, heads, W, b):
            d = H.shape[1]
            return H[heads] @ W[:, :d].T + E @ W[:, d:].T + b

        def _layer_norm(x, gamma, beta):
            mu = jnp.mean(x, axis=-1, keepdims=True)
            var = jnp.mean(jnp.square(x - mu), axis=-1, keepdims=True)
            return (x - mu) * jax.lax.rsqrt(var + LN_EPS) * gamma + beta
        key = jax.random.key(seed)
        k = jax.random.split(key, 8)
        H = jax.random.normal(k[0], (N_NODES, EMBED), dtype=jnp.float32)
        E = jax.random.normal(k[1], (N_EDGES, EMBED), dtype=jnp.float32)
        ht = jax.random.randint(k[2], (N_EDGES, 2), 0, N_NODES, dtype=jnp.int64)
        ht = ht.at[:N_NODES, 0].set(jnp.arange(N_NODES, dtype=jnp.int64))
        queries = jnp.zeros((1,), dtype=jnp.float32)
        lim = 1.0 / np.sqrt(2 * EMBED)
        W_fwd = jax.random.uniform(k[3], (EMBED, 2 * EMBED), jnp.float32, -lim, lim)
        b_fwd = jax.random.uniform(k[4], (EMBED,), jnp.float32, -lim, lim)
        W_back = jax.random.uniform(k[5], (EMBED, 2 * EMBED), jnp.float32, -lim, lim)
        b_back = jax.random.uniform(k[6], (EMBED,), jnp.float32, -lim, lim)
        gamma = jnp.ones((EMBED,), dtype=jnp.float32)
        beta = jnp.zeros((EMBED,), dtype=jnp.float32)
        return {'H': H, 'E': E, 'ht': ht, 'queries': queries, 'W_fwd': W_fwd, 'b_fwd': b_fwd, 'W_back': W_back, 'b_back': b_back, 'gamma': gamma, 'beta': beta}
    _L1_gnn_all = _L1_gnn_setup()
    _L1_gnn_in = {k: v for k, v in _L1_gnn_all.items() if k in ('queries', 'W_fwd', 'b_fwd', 'W_back', 'b_back', 'gamma', 'beta')}
    del _L1_gnn_all

    def _L2_gnn_setup():
        import jax, jax.numpy as jnp
        import numpy as np
        N = 12500
        E = 200000
        D_IN = 128
        D_HID = 128
        D_OUT = 128
        HEADS = 4
        NEG_SLOPE = 0.2

        def _gat_conv(x, W, a_src, a_dst, bias, src, dst, n_nodes):
            H, C = a_src.shape
            h = (x @ W).reshape(n_nodes, H, C)
            s_src = jnp.einsum('nhc,hc->nh', h, a_src)
            s_dst = jnp.einsum('nhc,hc->nh', h, a_dst)
            e = s_src[src] + s_dst[dst]
            e = jnp.where(e > 0, e, NEG_SLOPE * e)
            e_max = jax.ops.segment_max(e, dst, num_segments=n_nodes)
            e_exp = jnp.exp(e - e_max[dst])
            denom = jax.ops.segment_sum(e_exp, dst, num_segments=n_nodes)
            alpha = e_exp / denom[dst]
            msg = alpha[:, :, None] * h[src]
            out = jax.ops.segment_sum(msg, dst, num_segments=n_nodes)
            return out.reshape(n_nodes, H * C) + bias
        key = jax.random.key(seed)
        ks = jax.random.split(key, 16)
        ch1 = D_HID // HEADS
        ch2 = D_OUT // HEADS
        inp = {'x': jax.random.normal(ks[0], (N, D_IN), dtype=jnp.float32), 'edge_index': jax.random.randint(ks[1], (2, E), 0, N, dtype=jnp.int64), 'W1': jax.random.normal(ks[2], (D_IN, HEADS * ch1), dtype=jnp.float32) * 0.05, 'a1_src': jax.random.normal(ks[3], (HEADS, ch1), dtype=jnp.float32) * 0.05, 'a1_dst': jax.random.normal(ks[4], (HEADS, ch1), dtype=jnp.float32) * 0.05, 'b1': jnp.zeros((HEADS * ch1,), dtype=jnp.float32), 'W2': jax.random.normal(ks[5], (D_HID, HEADS * ch2), dtype=jnp.float32) * 0.05, 'a2_src': jax.random.normal(ks[6], (HEADS, ch2), dtype=jnp.float32) * 0.05, 'a2_dst': jax.random.normal(ks[7], (HEADS, ch2), dtype=jnp.float32) * 0.05, 'b2': jnp.zeros((HEADS * ch2,), dtype=jnp.float32), 'Wr': jax.random.normal(ks[8], (D_IN, D_OUT), dtype=jnp.float32) * 0.05, 'br': jnp.zeros((D_OUT,), dtype=jnp.float32)}
        return inp
    _L2_gnn_all = _L2_gnn_setup()
    _L2_gnn_in = {k: v for k, v in _L2_gnn_all.items() if k in ('W1', 'a1_src', 'a1_dst', 'b1', 'W2', 'a2_src', 'a2_dst', 'b2', 'Wr', 'br')}
    del _L2_gnn_all

    def _L3_gnn_setup():
        import jax, jax.numpy as jnp
        import numpy as np
        N = 6250
        E = 100000
        F = 128
        COMP_RATIO = 4

        def _sage_mean(x, src, dst, w_self, w_neigh, b):
            n = x.shape[0]
            msg = x[src]
            summed = jax.ops.segment_sum(msg, dst, num_segments=n)
            deg = jax.ops.segment_sum(jnp.ones((src.shape[0],), x.dtype), dst, num_segments=n)
            mean = summed / jnp.maximum(deg, 1.0)[:, None]
            return x @ w_self + mean @ w_neigh + b
        key = jax.random.key(seed)
        ks = jax.random.split(key, 16)
        s = 1.0 / np.sqrt(F)
        inp = {'x': jax.random.normal(ks[0], (N, F), jnp.float32), 'src': jax.random.randint(ks[1], (E,), 0, N, jnp.int32), 'dst': jax.random.randint(ks[2], (E,), 0, N, jnp.int32), 'ws1': jax.random.normal(ks[3], (F, F), jnp.float32) * s, 'wn1': jax.random.normal(ks[4], (F, F), jnp.float32) * s, 'b1': jnp.zeros((F,), jnp.float32), 'ws2': jax.random.normal(ks[5], (F, F), jnp.float32) * s, 'wn2': jax.random.normal(ks[6], (F, F), jnp.float32) * s, 'b2': jnp.zeros((F,), jnp.float32), 'w_score': jax.random.normal(ks[7], (F, 1), jnp.float32) * s, 'b_score': jnp.zeros((1,), jnp.float32), 'wu1': jax.random.normal(ks[8], (F, F), jnp.float32) * s, 'wnu1': jax.random.normal(ks[9], (F, F), jnp.float32) * s, 'bu1': jnp.zeros((F,), jnp.float32), 'wu2': jax.random.normal(ks[10], (F, F), jnp.float32) * s, 'wnu2': jax.random.normal(ks[11], (F, F), jnp.float32) * s, 'bu2': jnp.zeros((F,), jnp.float32)}
        return inp
    _L3_gnn_all = _L3_gnn_setup()
    _L3_gnn_in = {k: v for k, v in _L3_gnn_all.items() if k in ('ws1', 'wn1', 'b1', 'ws2', 'wn2', 'b2', 'w_score', 'b_score', 'wu1', 'wnu1', 'bu1', 'wu2', 'wnu2', 'bu2')}
    del _L3_gnn_all
    return {'x': x, 'src': src, 'dst': dst, 'edge_attr_128': edge_attr_128, 'L0_gnn_W': _L0_gnn_in['W'], 'L0_gnn_b': _L0_gnn_in['b'], 'L1_gnn_queries': _L1_gnn_in['queries'], 'L1_gnn_W_fwd': _L1_gnn_in['W_fwd'], 'L1_gnn_b_fwd': _L1_gnn_in['b_fwd'], 'L1_gnn_W_back': _L1_gnn_in['W_back'], 'L1_gnn_b_back': _L1_gnn_in['b_back'], 'L1_gnn_gamma': _L1_gnn_in['gamma'], 'L1_gnn_beta': _L1_gnn_in['beta'], 'L2_gnn_W1': _L2_gnn_in['W1'], 'L2_gnn_a1_src': _L2_gnn_in['a1_src'], 'L2_gnn_a1_dst': _L2_gnn_in['a1_dst'], 'L2_gnn_b1': _L2_gnn_in['b1'], 'L2_gnn_W2': _L2_gnn_in['W2'], 'L2_gnn_a2_src': _L2_gnn_in['a2_src'], 'L2_gnn_a2_dst': _L2_gnn_in['a2_dst'], 'L2_gnn_b2': _L2_gnn_in['b2'], 'L2_gnn_Wr': _L2_gnn_in['Wr'], 'L2_gnn_br': _L2_gnn_in['br'], 'L3_gnn_ws1': _L3_gnn_in['ws1'], 'L3_gnn_wn1': _L3_gnn_in['wn1'], 'L3_gnn_b1': _L3_gnn_in['b1'], 'L3_gnn_ws2': _L3_gnn_in['ws2'], 'L3_gnn_wn2': _L3_gnn_in['wn2'], 'L3_gnn_b2': _L3_gnn_in['b2'], 'L3_gnn_w_score': _L3_gnn_in['w_score'], 'L3_gnn_b_score': _L3_gnn_in['b_score'], 'L3_gnn_wu1': _L3_gnn_in['wu1'], 'L3_gnn_wnu1': _L3_gnn_in['wnu1'], 'L3_gnn_bu1': _L3_gnn_in['bu1'], 'L3_gnn_wu2': _L3_gnn_in['wu2'], 'L3_gnn_wnu2': _L3_gnn_in['wnu2'], 'L3_gnn_bu2': _L3_gnn_in['bu2']}

def reference(x, src, dst, edge_attr_128, L0_gnn_W, L0_gnn_b, L1_gnn_queries, L1_gnn_W_fwd, L1_gnn_b_fwd, L1_gnn_W_back, L1_gnn_b_back, L1_gnn_gamma, L1_gnn_beta, L2_gnn_W1, L2_gnn_a1_src, L2_gnn_a1_dst, L2_gnn_b1, L2_gnn_W2, L2_gnn_a2_src, L2_gnn_a2_dst, L2_gnn_b2, L2_gnn_Wr, L2_gnn_br, L3_gnn_ws1, L3_gnn_wn1, L3_gnn_b1, L3_gnn_ws2, L3_gnn_wn2, L3_gnn_b2, L3_gnn_w_score, L3_gnn_b_score, L3_gnn_wu1, L3_gnn_wnu1, L3_gnn_bu1, L3_gnn_wu2, L3_gnn_wnu2, L3_gnn_bu2):
    import jax
    import jax.numpy as jnp

    def _L0_gnn_ref(x, W, b, src, dst):
        import jax, jax.numpy as jnp
        import numpy as np
        N_NODES = 6250
        N_EDGES = 75000
        D = 128
        N = x.shape[0]
        neigh_sum = jax.ops.segment_sum(x[src], dst, num_segments=N)
        deg = jax.ops.segment_sum(jnp.ones_like(src, dtype=x.dtype), dst, num_segments=N)
        mean = neigh_sum / jnp.maximum(deg, 1.0)[:, None]
        neigh_agg = jnp.where(deg[:, None] > 0, mean, x)
        h = jnp.concatenate([x, neigh_agg], axis=-1)
        return jax.nn.relu(h @ W.T + b)

    def _L1_gnn_ref(H, E, ht, queries, W_fwd, b_fwd, W_back, b_back, gamma, beta):
        import jax, jax.numpy as jnp
        import numpy as np
        N_NODES = 12500
        N_EDGES = 200000
        EMBED = 128
        LN_EPS = 1e-05
        NEG_SLOPE = 0.01

        def _calc_messages(H, E, heads, W, b):
            d = H.shape[1]
            return H[heads] @ W[:, :d].T + E @ W[:, d:].T + b

        def _layer_norm(x, gamma, beta):
            mu = jnp.mean(x, axis=-1, keepdims=True)
            var = jnp.mean(jnp.square(x - mu), axis=-1, keepdims=True)
            return (x - mu) * jax.lax.rsqrt(var + LN_EPS) * gamma + beta
        n = H.shape[0]
        messages_fwd = _calc_messages(H, E, ht[:, 0], W_fwd, b_fwd)
        messages_back = _calc_messages(H, E, ht[:, 1], W_back, b_back)
        msg_dst = jnp.concatenate([ht[:, 1], ht[:, 0]])
        messages = jnp.concatenate([messages_fwd, messages_back], axis=0)
        agg = jax.ops.segment_sum(messages, msg_dst, num_segments=n)
        counts = jax.ops.segment_sum(jnp.ones((msg_dst.shape[0],), dtype=messages.dtype), msg_dst, num_segments=n)
        agg = agg / counts[:, None]
        out = _layer_norm(jax.nn.leaky_relu(agg, NEG_SLOPE) + H, gamma, beta)
        return out

    def _L2_gnn_ref(x, edge_index, W1, a1_src, a1_dst, b1, W2, a2_src, a2_dst, b2, Wr, br):
        import jax, jax.numpy as jnp
        import numpy as np
        N = 12500
        E = 200000
        D_IN = 128
        D_HID = 128
        D_OUT = 128
        HEADS = 4
        NEG_SLOPE = 0.2

        def _gat_conv(x, W, a_src, a_dst, bias, src, dst, n_nodes):
            H, C = a_src.shape
            h = (x @ W).reshape(n_nodes, H, C)
            s_src = jnp.einsum('nhc,hc->nh', h, a_src)
            s_dst = jnp.einsum('nhc,hc->nh', h, a_dst)
            e = s_src[src] + s_dst[dst]
            e = jnp.where(e > 0, e, NEG_SLOPE * e)
            e_max = jax.ops.segment_max(e, dst, num_segments=n_nodes)
            e_exp = jnp.exp(e - e_max[dst])
            denom = jax.ops.segment_sum(e_exp, dst, num_segments=n_nodes)
            alpha = e_exp / denom[dst]
            msg = alpha[:, :, None] * h[src]
            out = jax.ops.segment_sum(msg, dst, num_segments=n_nodes)
            return out.reshape(n_nodes, H * C) + bias
        n_nodes = x.shape[0]
        loops = jnp.arange(n_nodes, dtype=edge_index.dtype)
        src = jnp.concatenate([edge_index[0], loops])
        dst = jnp.concatenate([edge_index[1], loops])
        h1 = _gat_conv(x, W1, a1_src, a1_dst, b1, src, dst, n_nodes)
        h1 = jax.nn.relu(h1)
        h2 = _gat_conv(h1, W2, a2_src, a2_dst, b2, src, dst, n_nodes)
        return h2 + x @ Wr + br

    def _L3_gnn_ref(x, src, dst, ws1, wn1, b1, ws2, wn2, b2, w_score, b_score, wu1, wnu1, bu1, wu2, wnu2, bu2):
        import jax, jax.numpy as jnp
        import numpy as np
        N = 6250
        E = 100000
        F = 128
        COMP_RATIO = 4

        def _sage_mean(x, src, dst, w_self, w_neigh, b):
            n = x.shape[0]
            msg = x[src]
            summed = jax.ops.segment_sum(msg, dst, num_segments=n)
            deg = jax.ops.segment_sum(jnp.ones((src.shape[0],), x.dtype), dst, num_segments=n)
            mean = summed / jnp.maximum(deg, 1.0)[:, None]
            return x @ w_self + mean @ w_neigh + b
        n = x.shape[0]
        k = max(1, n // COMP_RATIO)
        h = jax.nn.relu(_sage_mean(x, src, dst, ws1, wn1, b1))
        h = _sage_mean(h, src, dst, ws2, wn2, b2)
        score = jax.nn.sigmoid(h @ w_score + b_score)[:, 0]
        _, idx = jax.lax.top_k(score, k)
        compressed = h[idx]
        new_val = jnp.zeros((n, h.shape[1]), h.dtype).at[idx].set(compressed)
        d = jax.nn.relu(_sage_mean(new_val, src, dst, wu1, wnu1, bu1))
        d = _sage_mean(d, src, dst, wu2, wnu2, bu2)
        return d
    edge_index = jnp.stack([src, dst])
    edge_index_t = jnp.stack([src, dst], axis=1)
    x = _layernorm(x + _L0_gnn_ref(x, L0_gnn_W, L0_gnn_b, src, dst), axis=-1)
    x = _layernorm(x + _L1_gnn_ref(x, edge_attr_128, edge_index_t, L1_gnn_queries, L1_gnn_W_fwd, L1_gnn_b_fwd, L1_gnn_W_back, L1_gnn_b_back, L1_gnn_gamma, L1_gnn_beta), axis=-1)
    x = _layernorm(x + _L2_gnn_ref(x, edge_index, L2_gnn_W1, L2_gnn_a1_src, L2_gnn_a1_dst, L2_gnn_b1, L2_gnn_W2, L2_gnn_a2_src, L2_gnn_a2_dst, L2_gnn_b2, L2_gnn_Wr, L2_gnn_br), axis=-1)
    x = _layernorm(x + _L3_gnn_ref(x, src, dst, L3_gnn_ws1, L3_gnn_wn1, L3_gnn_b1, L3_gnn_ws2, L3_gnn_wn2, L3_gnn_b2, L3_gnn_w_score, L3_gnn_b_score, L3_gnn_wu1, L3_gnn_wnu1, L3_gnn_bu1, L3_gnn_wu2, L3_gnn_wnu2, L3_gnn_bu2), axis=-1)
    return x

_drawn_inputs = setup_inputs


def setup_inputs(seed=0):
    import zlib

    import numpy as np

    out = dict(_drawn_inputs(seed))
    spreads = {'L1_gnn_gamma': (1.0, 0.2),
     'L1_gnn_beta': (0.0, 0.1),
     'L2_gnn_b1': (0.0, 0.1),
     'L2_gnn_b2': (0.0, 0.1),
     'L2_gnn_br': (0.0, 0.1),
     'L3_gnn_b1': (0.0, 0.1),
     'L3_gnn_b2': (0.0, 0.1),
     'L3_gnn_bu1': (0.0, 0.1),
     'L3_gnn_bu2': (0.0, 0.1)}
    factors = {'L0_gnn_b': 3.113,
     'L1_gnn_b_fwd': 2.856,
     'L1_gnn_b_back': 2.84,
     'L2_gnn_a1_src': 4.53,
     'L2_gnn_a1_dst': 50.605,
     'L2_gnn_a2_src': 64.0,
     'L2_gnn_a2_dst': 64.0}
    for name, (base, spread) in spreads.items():
        noise = np.random.default_rng([zlib.crc32(name.encode()), seed]).standard_normal(out[name].shape)
        drawn = base * np.exp(spread * noise) if base else spread * noise
        out[name] = jnp.asarray(drawn.astype(out[name].dtype))
    for name, factor in factors.items():
        out[name] = (out[name] * factor).astype(out[name].dtype)
    return out
```

```python
from contextlib import ExitStack

import concourse.bass as bass
from concourse import mybir

ALU = mybir.AluOpType
ACT = mybir.ActivationFunctionType
F32 = mybir.dt.float32
BF16 = mybir.dt.bfloat16
I32 = mybir.dt.int32
AX_X = mybir.AxisListType.X
RMAX = bass.bass_isa.ReduceOp.max

P = 128
G = 4
RING = 8
BLOCK = RING * G
QUAD = 4
SEVEN = 7
HB = 16
FILL = 512
LN_EPS = 1e-5
BY_DST, BY_SRC = 0, 1
FAR = -1e30


class Count:

    def __init__(self, sem):
        self.sem, self.base, self.k, self.at, self.per = sem, 0, 0, None, 0

    def loop(self, at, per_turn):
        self.base += self.k
        self.at, self.k, self.per = at, 0, per_turn

    def end(self, trips):
        assert self.k == self.per, (self.k, self.per)
        self.base += trips * self.per
        self.at, self.k = None, 0

    def by(self, ins, n=1):
        self.k += n
        return ins.then_inc(self.sem, n)

    def settle(self, eng, alone=None):
        v = self.base + self.k
        hold(eng, self.sem, v if self.at is None else self.at * self.per + v, alone)


def hold(eng, sem, value, alone):
    eng.wait_ge(sem, value)
    if alone is not None:
        eng.sem_inc(alone, 1)


def bc(ap, axis, shape):
    return ap.unsqueeze(axis).broadcast_to(shape)


def gnn_kernel(nc, a, out, stop_after=None):
    N, D = a["x"].shape
    E = a["src"].shape[0]
    NT = -(-N // (P * SEVEN)) * SEVEN
    NP = NT * P
    HI = NT + 1
    BODY = 2 * QUAD
    TC = -(-E // (P * HB)) * HB
    FULL, REST = divmod(E, TC)
    COLS = -(-(E + NT * G + 2 * BLOCK) // FILL) * FILL + FILL
    DUMMY_NODE, DUMMY_EDGE = NP, 1 << 20
    HEADS, CH = a["L2_gnn_a1_src"].shape
    TOP = max(1, N // 4)
    H_TURNS, J_TURNS, R_TURNS = TC // HB, TC // BODY, NT // SEVEN
    assert D == P and HEADS * CH == D and P * COLS + P * HB < 1 << 24 and E < DUMMY_EDGE

    with ExitStack() as ctx:
        def sb(name, shape, dt=F32):
            return ctx.enter_context(nc.sbuf_tensor(name, shape, dt))

        def psum(name, shape, dt=F32):
            return ctx.enter_context(nc.psum_tensor(name, shape, dt))

        def sem(name):
            return ctx.enter_context(nc.semaphore(name))

        def dram(name, shape, dt=F32):
            return nc.dram_tensor(name, shape, dt).ap()

        slots = [dram(f"slots_{k}", (P * COLS + P * HB, 2), I32) for k in ("by_dst", "by_src")]
        nodes_by_place = dram("nodes_by_place", (NP, 4))

        iota_b = sb("iota_b", [P, P], BF16)
        iota_f = sb("iota_f", [P, P])
        part_f = sb("part_f", [P, 1])
        earlier = sb("earlier", [P, P], BF16)
        earlier_f = sb("earlier_f", [P, P])
        ident_b = sb("ident_b", [P, P], BF16)
        ident = sb("ident", [P, P])
        ones_b = sb("ones_b", [P, 1], BF16)
        ones = sb("ones", [P, P])
        zeros_b = sb("zeros_b", [P, P], BF16)

        bank = [psum(f"bank{i}", [P, 512]) for i in range(8)]

        s_const = sem("s_const")
        s_dve = sem("s_dve")
        s_meta = sem("s_meta")
        s_binned = sem("s_binned")
        s_held_dve = sem("s_held_dve")
        s_held_pool = sem("s_held_pool")

        groups = sb("groups", [P, 2, NT], I32)
        first = sb("first", [P, 2, NT], I32)
        total = sb("total", [P, 2, 2], I32)
        by_place = sb("by_place", [P, NT, 4])
        st = Count(s_dve)

        with ExitStack() as binning:
            def sbb(name, shape, dt=F32):
                return binning.enter_context(nc.sbuf_tensor(name, shape, dt))

            def bsem(name):
                return binning.enter_context(nc.semaphore(name))

            ends = sbb("ends", [P, 2, TC], I32)
            scratch = sbb("scratch", [P, 2, TC], I32)
            lo = sbb("lo", [P, 2, TC], BF16)
            hi = sbb("hi", [P, 2, TC], BF16)
            edge_no = sbb("edge_no", [P, TC], I32)
            is_lo = [sbb(f"is_lo{k}", [P, HB, P], BF16) for k in range(2)]
            is_hi = [sbb(f"is_hi{k}", [P, HB, HI], BF16) for k in range(2)]
            degree = sbb("degree", [P, 2, HI])
            node_rows = sbb("node_rows", [P, NT, 4])
            bin_f = sbb("bin_f", [P, NT])
            is_bin = sbb("is_bin", [P, SEVEN, P], BF16)
            bin_T = sbb("bin_T", [P, SEVEN, P], BF16)
            bin_Tf = sbb("bin_Tf", [P, SEVEN, P])
            bin_same = sbb("bin_same", [P, SEVEN, P], BF16)
            bin_count = [sbb(f"bin_count{i}", [P, NT + 1]) for i in range(2)]
            bin_base = sbb("bin_base", [P, SEVEN])
            place_f = sbb("place_f", [P, NT])
            place_i = sbb("place_i", [P, NT], I32)
            place_x = sbb("place_x", [P, NT], I32)
            place_part = sbb("place_part", [P, NT])
            place_tile = sbb("place_tile", [P, NT])
            tile_pick = sbb("tile_pick", [P, NT, NT])
            most = sbb("most", [P, 2, NT])
            most_all = sbb("most_all", [P, 2, NT])
            count_f = sbb("count_f", [P, 2, NT])
            scan = [sbb(f"scan{i}", [P, 2, NT + 1]) for i in range(2)]
            tot_i = sbb("tot_i", [P, 2, 2], I32)
            running = sbb("running", [P, 2, 2, HI])
            fill = sbb("fill", [P, FILL, 2], I32)
            q_lo = [[sbb(f"q_lo{b}{k}", [P, QUAD, P], BF16) for k in range(2)] for b in range(2)]
            q_hi = [[sbb(f"q_hi{b}{k}", [P, QUAD, HI], BF16) for k in range(2)] for b in range(2)]
            lo_T = [[sbb(f"lo_T{b}{k}", [P, QUAD, P], BF16) for k in range(2)] for b in range(2)]
            lo_Tf = [[sbb(f"lo_Tf{b}{k}", [P, QUAD, P]) for k in range(2)] for b in range(2)]
            same = [sbb(f"same{k}", [P, QUAD, P], BF16) for k in range(2)]
            picked = sbb("picked", [P, 2, QUAD, 2, HI])
            found = sbb("found", [P, 2, QUAD, 2])
            slot_no = [sbb(f"slot_no{b}", [P, 2, QUAD], I32) for b in range(2)]
            record = [sbb(f"record{b}", [P, 2, QUAD, 2], I32) for b in range(2)]

            s_ends = bsem("s_ends")
            s_onehot = bsem("s_onehot")
            s_hist = bsem("s_hist")
            s_bins = bsem("s_bins")
            s_binsum = bsem("s_binsum")
            s_binsum_read = bsem("s_binsum_read")
            s_bincol = bsem("s_bincol")
            s_binT = bsem("s_binT")
            s_binTc = bsem("s_binTc")
            s_binE = bsem("s_binE")
            s_binM = bsem("s_binM")
            s_rank = bsem("s_rank")
            s_places = bsem("s_places")
            s_rows_out = bsem("s_rows_out")
            s_rows_in = bsem("s_rows_in")
            s_most = bsem("s_most")
            s_most_all = bsem("s_most_all")
            s_filled = bsem("s_filled")
            s_fill_done = bsem("s_fill_done")
            s_quad = [bsem(f"s_quad{k}") for k in range(2)]
            s_T = [bsem(f"s_T{k}") for k in range(2)]
            s_Tcopy = [bsem(f"s_Tcopy{k}") for k in range(2)]
            s_same = [bsem(f"s_same{k}") for k in range(2)]
            s_mask = [bsem(f"s_mask{k}") for k in range(2)]
            s_run = [bsem(f"s_run{k}") for k in range(2)]
            s_runcopy = [bsem(f"s_runcopy{k}") for k in range(2)]
            s_found = [bsem(f"s_found{k}") for k in range(2)]
            s_taken = [bsem(f"s_taken{k}") for k in range(2)]
            s_record = bsem("s_record")
            s_record_free = bsem("s_record_free")
            s_scatter = [bsem(f"s_scatter{b}") for b in range(2)]

            ps_hist = [bank[k][:, 0:HI] for k in range(2)]
            ps_count = bank[2][:, 0:SEVEN]
            ps_start = bank[3][:, 0:1]
            ps_binT = bank[4][:].bitcast(BF16)[:, 0:SEVEN * P].rearrange("p (c f) -> p c f", c=SEVEN)
            ps_binE = [bank[5][:].rearrange("p (c f) -> p c f", c=4), bank[6][:].rearrange("p (c f) -> p c f", c=4)]
            ps_rank = bank[7][:, 0:SEVEN]
            ps_T = [bank[k][:].bitcast(BF16)[:, 0:QUAD * P].rearrange("p (c f) -> p c f", c=QUAD) for k in range(2)]
            ps_same = [bank[2 + k][:].rearrange("p (c f) -> p c f", c=QUAD) for k in range(2)]
            ps_found = [bank[4 + k][:, 0:QUAD * 2 * HI].rearrange("p (c f) -> p c f", c=QUAD) for k in range(2)]
            ps_run = [bank[6 + k][:, 0:HI] for k in range(2)]

            blk = binning.enter_context(nc.Block())

            @blk.sync
            def _(sp):
                sp.wait_ge(s_const, 1)
                for k, name in ((BY_DST, "dst"), (BY_SRC, "src")):
                    sp.dma_start(ends[0:FULL, k, :], a[name][0:FULL * TC].rearrange("(p c) -> p c", c=TC)
                                 ).then_inc(s_ends, 16)
                    sp.dma_start(ends[FULL:FULL + 1, k, 0:REST],
                                 a[name][FULL * TC:E].rearrange("(p c) -> p c", p=1)).then_inc(s_ends, 16)
                sp.wait_ge(s_rows_out, 16 * NT)
                sp.dma_start(by_place[:], nodes_by_place.rearrange("(t p) w -> p t w", p=P)).then_inc(s_rows_in, 16)
                sp.wait_ge(s_meta, 1)
                fills = [sp.value_load(total[0:1, k, 1:2], min_val=1, max_val=COLS // FILL) for k in range(2)]
                for k in range(2):
                    table = slots[k][0:P * COLS, :].rearrange("(p c) w -> p c w", p=P)
                    with sp.Fori(0, fills[k]) as i:
                        sp.dma_start(table[:, bass.ds(i * FILL, FILL), :], fill[:]).then_inc(s_filled, 16)
                sp.wait_ge(s_filled, (fills[0] + fills[1]) * 16)
                sp.sem_inc(s_fill_done, 1)
                sp.sem_inc(s_record_free, 2)
                with sp.Fori(0, J_TURNS) as i:
                    for b in range(2):
                        sp.wait_ge(s_scatter[b], i * (16 * 2 * QUAD) + 16 * 2 * QUAD)
                        sp.sem_inc(s_record_free, 1)

            @blk.gpsimd
            def _(pool):
                nc.gpsimd.memset(ends[:], NT * P).then_inc(s_const, 1)
                nc.gpsimd.memset(ones[:], 1.0).then_inc(s_const, 1)
                nc.gpsimd.iota(iota_b[:], [[1, P]], base=0, channel_multiplier=0,
                               allow_small_or_imprecise_dtypes=True)
                nc.gpsimd.iota(iota_f[:], [[1, P]], base=0, channel_multiplier=0,
                               allow_small_or_imprecise_dtypes=True)
                nc.gpsimd.iota(part_f[:], [[0, 1]], base=0, channel_multiplier=1,
                               allow_small_or_imprecise_dtypes=True)
                nc.gpsimd.iota(edge_no[:], [[1, TC]], base=0, channel_multiplier=TC)
                nc.gpsimd.iota(node_rows[:, :, 2:4], [[P, NT], [0, 2]], base=0, channel_multiplier=1,
                               allow_small_or_imprecise_dtypes=True)
                nc.gpsimd.memset(ones_b[:], 1.0)
                nc.gpsimd.memset(zeros_b[:], 0.0)
                nc.gpsimd.memset(fill[:, :, 0:1], DUMMY_NODE)
                nc.gpsimd.memset(fill[:, :, 1:2], DUMMY_EDGE)
                pool.wait_ge(s_const, 2)
                for m, op in ((earlier, ALU.is_gt), (earlier_f, ALU.is_gt), (ident_b, ALU.is_equal),
                              (ident, ALU.is_equal)):
                    last = nc.gpsimd.affine_select(out=m[:], in_=ones[:], compare_op=op, fill=0.0, base=0,
                                                   pattern=[[1, P]], channel_multiplier=-1)
                last.then_inc(s_const, 1)
                pool.wait_ge(s_places, 1)
                for t in range(NT):
                    pool.indirect_dma_start(
                        out=nodes_by_place, out_offset=bass.IndirectOffsetOnAxis(ap=place_i[:, t:t + 1], axis=0),
                        in_=node_rows[:, t, :], in_offset=None).then_inc(s_rows_out, 16)
                pool.wait_ge(s_most, 1)
                nc.gpsimd.partition_all_reduce(most_all[:].rearrange("p a b -> p (a b)"),
                                               most[:].rearrange("p a b -> p (a b)"), P, RMAX).then_inc(s_most_all, 1)
                pool.wait_ge(s_fill_done, 1)
                with pool.Fori(0, J_TURNS) as i:
                    for b in range(2):
                        hold(pool, s_record, i * 2 + (b + 1), s_held_pool)
                        for k in range(2):
                            for q in range(QUAD):
                                pool.indirect_dma_start(
                                    out=slots[k],
                                    out_offset=bass.IndirectOffsetOnAxis(ap=slot_no[b][:, k, q:q + 1], axis=0),
                                    in_=record[b][:, k, q, :], in_offset=None).then_inc(s_scatter[b], 16)
                for b in range(2):
                    pool.wait_ge(s_scatter[b], 16 * 2 * QUAD * J_TURNS)
                pool.sem_inc(s_binned, 1)

            @blk.tensor
            def _(pe):
                pe.wait_ge(s_const, 3)
                for k in range(2):
                    nc.tensor.matmul(ps_hist[k], zeros_b[:], zeros_b[:, 0:HI], start=True, stop=False,
                                     skip_group_check=True)
                pe.sem_inc(s_hist, 2)
                with pe.Fori(0, H_TURNS) as i:
                    for k in range(2):
                        pe.wait_ge(s_onehot, i * 2 + (k + 1))
                        for c in range(HB):
                            mm = nc.tensor.matmul(ps_hist[k], is_lo[k][:, c, :], is_hi[k][:, c, :],
                                                  start=False, stop=False, skip_group_check=True)
                        mm.then_inc(s_hist, 1)
                pe.sem_inc(s_binsum, 1)
                with pe.Fori(0, R_TURNS) as i:
                    pe.wait_ge(s_bins, i + 1)
                    pe.wait_ge(s_binsum_read, i + 1)
                    for c in range(SEVEN):
                        mm = nc.tensor.matmul(ps_count[:, c:c + 1], is_bin[:, c, :], ones_b[:], start=True, stop=True)
                    mm.then_inc(s_binsum, 1)
                pe.wait_ge(s_bincol, 1)
                nc.tensor.matmul(ps_start, earlier_f[:], bin_count[0][:, NT:NT + 1], start=True,
                                 stop=True).then_inc(s_binsum, 1)
                pe.sem_inc(s_rank, 1)
                with pe.Fori(0, R_TURNS) as i:
                    pe.wait_ge(s_bins, i + (R_TURNS + 1))
                    for c in range(SEVEN):
                        mm = nc.tensor.transpose(ps_binT[:, c, :], is_bin[:, c, :], ident_b[:])
                    mm.then_inc(s_binT, 1)
                    pe.wait_ge(s_binTc, i + 1)
                    for c in range(SEVEN):
                        mm = nc.tensor.matmul(ps_binE[c // 4][:, c % 4, :], bin_T[:, c, :], bin_T[:, c, :],
                                              start=True, stop=True)
                    mm.then_inc(s_binE, 1)
                    pe.wait_ge(s_binM, i + 1)
                    for c in range(SEVEN):
                        nc.tensor.matmul(ps_rank[:, c:c + 1], bin_Tf[:, c, :], bin_base[:, c:c + 1],
                                         start=True, stop=False)
                        mm = nc.tensor.matmul(ps_rank[:, c:c + 1], bin_same[:, c, :], ones_b[:],
                                              start=False, stop=True)
                    mm.then_inc(s_rank, 1)
                pe.wait_ge(s_meta, 2)
                for k in range(2):
                    nc.tensor.matmul(ps_run[k], ident[:], running[:, k, 0, :], start=True, stop=False,
                                     skip_group_check=True)
                    pe.sem_inc(s_run[k], 2 * QUAD)
                with pe.Fori(0, J_TURNS) as i:
                    for b in range(2):
                        for k in range(2):
                            pe.wait_ge(s_quad[k], i * 2 + (b + 1))
                            pe.wait_ge(s_Tcopy[k], i * 2 + (b + 1))
                            for c in range(QUAD):
                                mm = nc.tensor.transpose(ps_T[k][:, c, :], q_lo[b][k][:, c, :], ident_b[:])
                            mm.then_inc(s_T[k], 1)
                    for b in range(2):
                        for k in range(2):
                            pe.wait_ge(s_Tcopy[k], i * 2 + (b + 2))
                            pe.wait_ge(s_mask[k], i * 2 + (b + 1))
                            for c in range(QUAD):
                                mm = nc.tensor.matmul(ps_same[k][:, c, :], lo_T[b][k][:, c, :], lo_T[b][k][:, c, :],
                                                      start=True, stop=True)
                            mm.then_inc(s_same[k], 1)
                        for k in range(2):
                            pe.wait_ge(s_mask[k], i * 2 + (b + 2))
                            pe.wait_ge(s_taken[k], i * 2 + (b + 1))
                        for c in range(QUAD):
                            for k in range(2):
                                pe.wait_ge(s_runcopy[k], i * (2 * QUAD) + (b * QUAD + c + 1))
                                nc.tensor.matmul(ps_found[k][:, c, :], lo_Tf[b][k][:, c, :],
                                                 running[:, k, :, :].rearrange("p a b -> p (a b)"),
                                                 start=True, stop=False, skip_group_check=True)
                                mm = nc.tensor.matmul(ps_found[k][:, c, 0:HI], same[k][:, c, :], q_hi[b][k][:, c, :],
                                                      start=False, stop=True, skip_group_check=True)
                                if c == QUAD - 1:
                                    mm.then_inc(s_found[k], 1)
                                nc.tensor.matmul(ps_run[k], q_lo[b][k][:, c, :], q_hi[b][k][:, c, :],
                                                 start=False, stop=False, skip_group_check=True).then_inc(s_run[k], 1)

            @blk.scalar
            def _(act):
                with act.Fori(0, R_TURNS) as i:
                    act.wait_ge(s_binT, i + 1)
                    act.wait_ge(s_rank, i + 1)
                    nc.scalar.copy(bin_T[:], ps_binT)
                    nc.scalar.copy(bin_Tf[:], ps_binT).then_inc(s_binTc, 1)
                for k in range(2):
                    act.sem_inc(s_Tcopy[k], 1)
                    act.sem_inc(s_runcopy[k], 1)
                with act.Fori(0, J_TURNS) as i:
                    for b in range(2):
                        for k in range(2):
                            act.wait_ge(s_T[k], i * 2 + (b + 1))
                            act.wait_ge(s_run[k], i * (2 * QUAD) + QUAD * (b + 1))
                            nc.scalar.copy(lo_T[b][k][:], ps_T[k])
                            nc.scalar.copy(lo_Tf[b][k][:], ps_T[k]).then_inc(s_Tcopy[k], 1)
                    for b in range(2):
                        for c in range(QUAD):
                            for k in range(2):
                                act.wait_ge(s_run[k], i * (2 * QUAD) + (2 * QUAD + b * QUAD + c + 1))
                                nc.scalar.copy(running[:, k, 0, :], ps_run[k]).then_inc(s_runcopy[k], 1)

            @blk.vector
            def _(dve):
                V = nc.vector
                dve.wait_ge(s_const, 3)
                dve.wait_ge(s_ends, 64)
                st.by(V.tensor_scalar(scratch[:], ends[:], P - 1, None, ALU.bitwise_and))
                st.settle(dve)
                st.by(V.tensor_copy(lo[:], scratch[:]))
                st.settle(dve)
                st.by(V.tensor_scalar(scratch[:], ends[:], 7, None, ALU.logical_shift_right))
                st.settle(dve)
                st.by(V.tensor_copy(hi[:], scratch[:]))
                st.settle(dve)

                with dve.Fori(0, H_TURNS) as i:
                    for k in range(2):
                        dve.wait_ge(s_hist, i * 2 + (k + 1))
                        V.tensor_tensor(is_lo[k][:], bc(lo[:, k, bass.ds(i * HB, HB)], 2, [P, HB, P]),
                                        bc(iota_b[:], 1, [P, HB, P]), ALU.is_equal)
                        V.tensor_tensor(is_hi[k][:], bc(hi[:, k, bass.ds(i * HB, HB)], 2, [P, HB, HI]),
                                        bc(iota_b[:, 0:HI], 1, [P, HB, HI]), ALU.is_equal).then_inc(s_onehot, 1)
                dve.wait_ge(s_hist, 2 * H_TURNS + 2)
                for k in range(2):
                    st.by(V.tensor_copy(degree[:, k, :], ps_hist[k]))
                st.settle(dve)
                st.by(V.tensor_tensor(bin_f[:], degree[:, 0, 0:NT], degree[:, 1, 0:NT], ALU.add))
                for k in range(2):
                    st.by(V.tensor_copy(node_rows[:, :, k], degree[:, k, 0:NT]))
                st.settle(dve)
                st.by(V.tensor_scalar(bin_f[:], bin_f[:], float(P - 1), -1.0, ALU.min, ALU.mult))
                st.settle(dve)
                st.by(V.tensor_scalar(bin_f[:], bin_f[:], float(P - 1), None, ALU.add))
                st.settle(dve)

                def bins(i, waits):
                    for s, v in waits:
                        dve.wait_ge(s, v)
                    V.tensor_tensor(is_bin[:], bc(bin_f[:, bass.ds(i * SEVEN, SEVEN)], 2, [P, SEVEN, P]),
                                    bc(iota_f[:], 1, [P, SEVEN, P]), ALU.is_equal).then_inc(s_bins, 1)

                dve.sem_inc(s_binsum_read, 1)
                with dve.Fori(0, R_TURNS) as i:
                    bins(i, [(s_binsum, i + 1)])
                    hold(dve, s_binsum, i + 2, s_held_dve)
                    V.tensor_copy(bin_count[1][:, bass.ds(i * SEVEN + 1, SEVEN)], ps_count).then_inc(s_binsum_read, 1)
                st.by(V.memset(bin_count[1][:, 0:1], 0.0))
                dve.wait_ge(s_binsum_read, R_TURNS + 1)
                st.settle(dve)
                now, step = 1, 1
                while step < NT + 1:
                    src, dst = bin_count[now], bin_count[1 - now]
                    st.by(V.tensor_copy(dst[:, 0:step], src[:, 0:step]))
                    st.by(V.tensor_tensor(dst[:, step:], src[:, step:], src[:, 0:NT + 1 - step], ALU.add))
                    st.settle(dve)
                    now, step = 1 - now, 2 * step
                if now == 1:
                    st.by(V.tensor_copy(bin_count[0][:], bin_count[1][:]))
                    st.settle(dve)
                dve.sem_inc(s_bincol, 1)
                dve.wait_ge(s_binsum, R_TURNS + 2)
                st.by(V.tensor_copy(bin_base[:, 0:1], ps_start))
                st.settle(dve)
                st.by(V.tensor_scalar(bin_count[1][:], bin_count[0][:], bin_base[:, 0:1], None, ALU.add))
                st.settle(dve)
                with dve.Fori(0, R_TURNS) as i:
                    bins(i, [(s_rank, i + 1)])
                    V.tensor_copy(bin_base[:], bin_count[1][:, bass.ds(i * SEVEN, SEVEN)])
                    dve.wait_ge(s_binE, i + 1)
                    V.tensor_tensor(bin_same[:, 0:4, :], ps_binE[0], bc(earlier_f[:], 1, [P, 4, P]), ALU.mult)
                    V.tensor_tensor(bin_same[:, 4:SEVEN, :], ps_binE[1][:, 0:SEVEN - 4, :],
                                    bc(earlier_f[:], 1, [P, SEVEN - 4, P]), ALU.mult).then_inc(s_binM, 1)
                    hold(dve, s_rank, i + 2, s_held_dve)
                    V.tensor_copy(place_f[:, bass.ds(i * SEVEN, SEVEN)], ps_rank).then_inc(s_binsum_read, 1)
                dve.wait_ge(s_binsum_read, 2 * R_TURNS + 1)
                V.tensor_copy(place_i[:], place_f[:]).then_inc(s_places, 1)
                dve.wait_ge(s_places, 1)
                st.by(V.tensor_scalar(place_x[:], place_i[:], P - 1, None, ALU.bitwise_and))
                st.settle(dve)
                st.by(V.tensor_copy(place_part[:], place_x[:]))
                st.settle(dve)
                st.by(V.tensor_scalar(place_x[:], place_i[:], 7, None, ALU.logical_shift_right))
                st.settle(dve)
                st.by(V.tensor_copy(place_tile[:], place_x[:]))
                st.settle(dve)
                dve.wait_ge(s_rows_in, 16)
                V.tensor_copy(most[:].rearrange("p k t -> p t k"), by_place[:, :, 0:2]).then_inc(s_most, 1)
                dve.wait_ge(s_most_all, 1)
                st.by(V.tensor_scalar(groups[:], most_all[:], float(G - 1), None, ALU.add))
                st.settle(dve)
                st.by(V.tensor_scalar(groups[:], groups[:], 2, None, ALU.logical_shift_right))
                st.settle(dve)
                st.by(V.tensor_scalar(groups[:], groups[:], 1, None, ALU.max))
                st.settle(dve)
                st.by(V.memset(scan[0][:], 0.0))
                st.settle(dve)
                st.by(V.tensor_copy(scan[0][:, :, 1:], groups[:]))
                st.settle(dve)
                now, step = 0, 1
                while step < NT + 1:
                    src, dst = scan[now], scan[1 - now]
                    st.by(V.tensor_copy(dst[:, :, 0:step], src[:, :, 0:step]))
                    st.by(V.tensor_tensor(dst[:, :, step:], src[:, :, step:], src[:, :, 0:NT + 1 - step], ALU.add))
                    st.settle(dve)
                    now, step = 1 - now, 2 * step
                begin = scan[now]
                st.by(V.tensor_copy(first[:], begin[:, :, 0:NT]))
                st.by(V.tensor_scalar(tot_i[:, :, 0:1], begin[:, :, NT:NT + 1], float(RING - 1), None, ALU.add))
                st.settle(dve)
                st.by(V.tensor_scalar(total[:, :, 0:1], tot_i[:, :, 0:1], -RING, None, ALU.bitwise_and))
                st.settle(dve)
                st.by(V.tensor_tensor(groups[:, :, NT - 1:NT], total[:, :, 0:1], first[:, :, NT - 1:NT], ALU.subtract))
                st.by(V.tensor_scalar(tot_i[:, :, 1:2], total[:, :, 0:1], float(G), float(BLOCK + FILL - 1),
                                      ALU.mult, ALU.add))
                st.settle(dve)
                st.by(V.tensor_scalar(total[:, :, 1:2], tot_i[:, :, 1:2], FILL.bit_length() - 1, None,
                                      ALU.logical_shift_right))
                st.settle(dve)
                dve.sem_inc(s_meta, 1)
                st.by(V.memset(running[:], 0.0))
                st.settle(dve)
                for k in range(2):
                    st.by(V.tensor_tensor(tile_pick[:], bc(place_tile[:], 2, [P, NT, NT]),
                                          bc(iota_f[:, 0:NT], 1, [P, NT, NT]), ALU.is_equal))
                    st.settle(dve)
                    st.by(V.tensor_tensor(tile_pick[:], tile_pick[:], bc(begin[:, k, 0:NT], 1, [P, NT, NT]), ALU.mult))
                    st.settle(dve)
                    st.by(V.tensor_reduce(running[:, k, 0, 0:NT], tile_pick[:], AX_X, ALU.add))
                    st.settle(dve)
                    st.by(V.tensor_scalar(count_f[:, k, :], place_part[:], float(COLS), None, ALU.mult))
                    st.settle(dve)
                    st.by(V.scalar_tensor_tensor(running[:, k, 0, 0:NT], running[:, k, 0, 0:NT], float(G),
                                                 count_f[:, k, :], ALU.mult, ALU.add))
                    st.by(V.tensor_copy(running[:, k, 1, 0:NT], place_f[:]))
                    st.by(V.memset(running[0:1, k, 0, NT:HI], float(P * COLS)))
                    st.settle(dve)
                dve.sem_inc(s_meta, 1)

                for k in range(2):
                    dve.sem_inc(s_mask[k], 1)
                    dve.sem_inc(s_taken[k], 1)
                with dve.Fori(0, J_TURNS) as i:
                    st.loop(i, 2 * 3)
                    for b in range(2):
                        for k in range(2):
                            dve.wait_ge(s_run[k], i * (2 * QUAD) + QUAD * (b + 1))
                            cols = bass.ds(i * BODY + b * QUAD, QUAD)
                            V.tensor_tensor(q_lo[b][k][:], bc(lo[:, k, cols], 2, [P, QUAD, P]),
                                            bc(iota_b[:], 1, [P, QUAD, P]), ALU.is_equal)
                            V.tensor_tensor(q_hi[b][k][:], bc(hi[:, k, cols], 2, [P, QUAD, HI]),
                                            bc(iota_b[:, 0:HI], 1, [P, QUAD, HI]), ALU.is_equal).then_inc(s_quad[k], 1)

                    def masks(b):
                        for k in range(2):
                            dve.wait_ge(s_same[k], i * 2 + (b + 1))
                            dve.wait_ge(s_run[k], i * (2 * QUAD) + QUAD * (b + 2))
                            V.tensor_tensor(same[k][:], ps_same[k], bc(earlier_f[:], 1, [P, QUAD, P]),
                                            ALU.mult).then_inc(s_mask[k], 1)

                    def finish(b):
                        for k in range(2):
                            dve.wait_ge(s_found[k], i * 2 + (b + 1))
                            V.tensor_tensor(picked[:, k], ps_found[k].rearrange("p c (w h) -> p c w h", w=2),
                                            bc(q_hi[b][k][:], 2, [P, QUAD, 2, HI]), ALU.mult).then_inc(s_taken[k], 1)
                        for k in range(2):
                            dve.wait_ge(s_taken[k], i * 2 + (b + 2))
                        st.by(V.tensor_reduce(found[:], picked[:], AX_X, ALU.add))
                        st.settle(dve)
                        dve.wait_ge(s_record_free, i * 2 + (b + 1))
                        st.by(V.tensor_copy(slot_no[b][:], found[:, :, :, 0]))
                        for k in range(2):
                            V.tensor_copy(record[b][:, k, :, 0], found[:, 1 - k, :, 1])
                        st.by(V.tensor_copy(record[b][:, :, :, 1],
                                            bc(edge_no[:, bass.ds(i * BODY + b * QUAD, QUAD)], 1, [P, 2, QUAD])))
                        st.settle(dve)
                        dve.sem_inc(s_record, 1)

                    masks(0)
                    masks(1)
                    finish(0)
                    finish(1)
                st.end(J_TURNS)

        if stop_after == "binning":
            return

        PHASES = [
            ("mean", "x0", BY_DST), ("rel_nodes_in", "x1", BY_DST), ("rel_edges_in", "edges", BY_DST),
            ("rel_nodes_out", "x1", BY_SRC), ("rel_edges_out", "edges", BY_SRC),
            ("att1", "att1", BY_DST), ("att2", "att2", BY_DST),
            ("pool1", "x3", BY_DST), ("pool2", "pool1", BY_DST), ("pool3", "top", BY_DST), ("pool4", "pool3", BY_DST)]
        W_ATT = D + 2 * HEADS
        W_HEAD = CH + 1
        tables = {n: dram(f"table_{n}", (NP + 1, W_ATT if n.startswith("att") else D))
                  for n in ("x0", "x1", "att1", "att2", "x3", "pool1", "top", "pool3")}

        X = sb("X", [P, NT, D])
        Y = sb("Y", [P, NT, D])
        H = sb("H", [P, NT, W_ATT])
        to_logit = sb("to_logit", [P, NT, HEADS])
        node_i = sb("node_i", [P, NT], I32)
        col = {n: sb(f"col_{n}", [P, NT]) for n in
               ("has_in", "w_mean", "w_self", "w_count", "w_deg", "real", "score", "chosen", "t0", "t1")}
        ring = sb("ring", [P, RING, G, W_ATT])
        ring_e = sb("ring_e", [P, RING, G, D])
        zeros = sb("zeros", [P, D])
        idx = [sb(f"idx{b}", [P, BLOCK // 2, 2], I32) for b in range(2)]
        empty_row = sb("empty_row", [1, W_ATT])
        MATS = {n: sb(f"w_{n}", [P, D * w]) for n, w in (
            ("mean_self", 1), ("mean_neigh", 1), ("fwd_node", 1), ("fwd_edge", 1), ("back_node", 1),
            ("back_edge", 1), ("att1", 2), ("att2", 1), ("s1", 1), ("n1", 1), ("s2", 1), ("n2", 1),
            ("us1", 1), ("un1", 1), ("us2", 1), ("un2", 1))}
        ROWS = {n: sb(f"r_{n}", [P, D]) for n in (
            "b_mean", "b_fwd", "b_back", "gamma", "beta", "b_att1", "b_att2", "b_res", "b_s1", "b_s2",
            "b_us1", "b_us2", "w_score")}
        att_rows = [sb(f"att_rows{i}", [P, 2, D]) for i in range(2)]
        b_score = sb("b_score", [P, 1])
        eps = sb("eps", [P, 1])

        acc = sb("acc", [P, D])
        part = sb("part", [P, D])
        ins = sb("ins", [P, 2, D])
        lhs = sb("lhs", [P, 2, P])
        y = sb("y", [P, D])
        z = sb("z", [P, D])
        stats = sb("stats", [P, 6])
        mean_var = sb("mean_var", [P, 2])
        std = sb("std", [P, 1])
        rstd = sb("rstd", [P, 1])
        logits = sb("logits", [P, G + 1, HEADS])
        raw = sb("raw", [P, G, HEADS])
        peak = sb("peak", [P, HEADS])
        shifted = sb("shifted", [P, G + 1, HEADS])
        probs = sb("probs", [P, G + 1, HEADS])
        weighted = sb("weighted", [P, G + 1, HEADS * W_HEAD])
        att_acc = sb("att_acc", [P, HEADS * W_HEAD])
        tile_logit = sb("tile_logit", [P, HEADS])
        r_sum = sb("r_sum", [P, HEADS])
        both = sb("both", [P, 2, D])
        thr = sb("thr", [P, 1], I32)
        cand = sb("cand", [P, 1], I32)
        bit = sb("bit", [P, 1], I32)
        keep = sb("keep", [P, 1], I32)
        cand_f = sb("cand_f", [P, 1])
        hits = sb("hits", [P, 1])
        need = sb("need", [P, 1])

        s_load = sem("s_load")
        s_ready = sem("s_ready")
        s_dummy = sem("s_dummy")
        s_x = sem("s_x")
        s_idx = [sem(f"s_idx{b}") for b in range(2)]
        s_ring = [sem(f"s_ring{j}") for j in range(RING)]
        s_landed = sem("s_landed")
        s_free = sem("s_free")
        s_sum = sem("s_sum")
        s_att = sem("s_att")
        s_shift = sem("s_shift")
        s_probs = sem("s_probs")
        s_in = sem("s_in")
        s_tr = sem("s_tr")
        s_lhs = sem("s_lhs")
        s_prod = sem("s_prod")
        s_var = sem("s_var")
        s_std = sem("s_std")
        s_tile = sem("s_tile")
        s_stored = sem("s_stored")
        s_count = sem("s_count")
        s_counted = sem("s_counted")
        s_logit = sem("s_logit")
        s_expd = sem("s_expd")
        s_last = sem("s_last")
        s_out = sem("s_out")

        ps_tr = bank[0][:, 0:2 * P].rearrange("p (j f) -> p j f", j=2)
        ps_prod = bank[1]
        ps_hits = bank[2][:, 0:1]

        PRODUCTS = {
            "mean": [("mean_self", "mean_neigh")], "rel_nodes_in": [("fwd_node",)], "rel_edges_in": [("fwd_edge",)],
            "rel_nodes_out": [("back_node",)], "rel_edges_out": [("back_edge",), ("att1",)],
            "att1": [("att2",)], "att2": [], "pool1": [("s1", "n1")], "pool2": [("s2", "n2")],
            "pool3": [("us1", "un1")], "pool4": [("us2", "un2")]}
        SCORE_BITS, NODE_BITS = 30, 13
        SEARCH = SCORE_BITS + 1 + NODE_BITS
        N_LOADS = 17 + 13 + 1 + 4
        ACT_STEPS = {"mean": "csw", "rel_nodes_in": "c", "rel_edges_in": "c", "rel_nodes_out": "c",
                     "rel_edges_out": "csscw", "att1": "cw", "att2": "sw", "pool1": "cw", "pool2": "c",
                     "pool3": "cw", "pool4": "cs"}
        STORES = {"mean": ("x1", X, D), "rel_edges_out": ("att1", H, W_ATT), "att1": ("att2", H, W_ATT),
                  "att2": ("x3", X, D), "pool1": ("pool1", H, D), "pool3": ("pool3", Y, D)}
        tile_mark, marks = {}, 0
        for name, _, _ in PHASES:
            tile_mark[name] = marks
            if name in STORES:
                marks += NT
            if name == "pool2":
                marks += 1
                tile_mark["top"] = marks
        STEPS = {"mean": 10, "rel_nodes_in": 3, "rel_edges_in": 3, "rel_nodes_out": 3, "rel_edges_out": 28,
                 "att1": 14, "att2": 12, "pool1": 5, "pool2": 7, "pool3": 5, "pool4": 9}
        if stop_after:
            PHASES = PHASES[:[p[0] for p in PHASES].index(stop_after) + 1]

        stored_by, stores, stored_before = {"x0": 16 + 16 * len(tables)}, 16 + 16 * len(tables), []
        for name, _, _ in PHASES:
            stored_before.append(stores)
            if name in STORES:
                stores += 16 * NT
                stored_by[STORES[name][0]] = stores
            if name == "pool2":
                stores += 16
                stored_by["top"] = stores

        def before(p):
            ks = [k for _, _, k in PHASES[:p]]
            return ks.count(BY_DST), ks.count(BY_SRC)

        def sizes(eng):
            return [eng.value_load(total[0:1, k, 0:1], min_val=2 * RING, max_val=(COLS - FILL) // G) for k in range(2)]

        def groups_before(eng, n, p, only=None):
            ks = [k for name, _, k in PHASES[:p] if only is None or name.startswith("att") == only]
            return eng.snap(n[0] * ks.count(BY_DST) + n[1] * ks.count(BY_SRC))

        blk = ctx.enter_context(nc.Block())

        @blk.sync
        def _(sp):
            loads = [
                (MATS["mean_self"], a["W0T"][0:D, :]), (MATS["mean_neigh"], a["W0T"][D:2 * D, :]),
                (MATS["fwd_node"], a["WfT"][0:D, :]), (MATS["fwd_edge"], a["WfT"][D:2 * D, :]),
                (MATS["back_node"], a["WbT"][0:D, :]), (MATS["back_edge"], a["WbT"][D:2 * D, :]),
                (MATS["att2"], a["L2_gnn_W2"]),
                (MATS["s1"], a["L3_gnn_ws1"]), (MATS["n1"], a["L3_gnn_wn1"]), (MATS["s2"], a["L3_gnn_ws2"]),
                (MATS["n2"], a["L3_gnn_wn2"]), (MATS["us1"], a["L3_gnn_wu1"]), (MATS["un1"], a["L3_gnn_wnu1"]),
                (MATS["us2"], a["L3_gnn_wu2"]), (MATS["un2"], a["L3_gnn_wnu2"])]
            for dst, src in loads:
                sp.dma_start(dst[:], src).then_inc(s_load, 16)
            sp.dma_start(MATS["att1"][:, 0:D], a["L2_gnn_W1"]).then_inc(s_load, 16)
            sp.dma_start(MATS["att1"][:, D:2 * D], a["L2_gnn_Wr"]).then_inc(s_load, 16)
            rows = [("b_mean", "L0_gnn_b"), ("b_fwd", "L1_gnn_b_fwd"), ("b_back", "L1_gnn_b_back"),
                    ("gamma", "L1_gnn_gamma"), ("beta", "L1_gnn_beta"), ("b_att1", "L2_gnn_b1"),
                    ("b_att2", "L2_gnn_b2"), ("b_res", "L2_gnn_br"), ("b_s1", "L3_gnn_b1"), ("b_s2", "L3_gnn_b2"),
                    ("b_us1", "L3_gnn_bu1"), ("b_us2", "L3_gnn_bu2")]
            for n, src in rows:
                sp.dma_start(ROWS[n][:], a[src].partition_broadcast(P)).then_inc(s_load, 16)
            sp.dma_start(ROWS["w_score"][:], a["L3_gnn_w_score"].rearrange("d o -> (d o)").partition_broadcast(P)
                         ).then_inc(s_load, 16)
            sp.dma_start(b_score[:], a["L3_gnn_b_score"].partition_broadcast(P)).then_inc(s_load, 16)
            for i in range(2):
                for j, end in enumerate(("src", "dst")):
                    sp.dma_start(att_rows[i][:, j, :],
                                 a[f"L2_gnn_a{i + 1}_{end}"].rearrange("h c -> (h c)").partition_broadcast(P)
                                 ).then_inc(s_load, 16)
            sp.wait_ge(s_dummy, 2)
            for n, t in tables.items():
                sp.dma_start(t[NP:NP + 1, :], empty_row[:, 0:t.shape[1]]).then_inc(s_stored, 16)
            sp.wait_ge(s_x, 16 * NT)
            sp.dma_start(tables["x0"][0:NP, :].rearrange("(t p) w -> p t w", p=P), X[:]).then_inc(s_stored, 16)

            n = sizes(sp)
            for p, (name, _, k) in enumerate(PHASES):
                base = groups_before(sp, n, p)
                table = slots[k][0:P * COLS, :].rearrange("(p c) w -> p c w", p=P)

                def load(turn, b):
                    sp.dma_start(idx[b][:], table[:, bass.ds(turn * BLOCK + b * (BLOCK // 2), BLOCK // 2), :]
                                 ).then_inc(s_idx[b], 16)

                def report(turn, b):
                    for j in range(b * RING // 2, (b + 1) * RING // 2):
                        sp.wait_ge(s_ring[j], (base + turn * RING) * (16 * G // RING) + 16 * G)
                        sp.sem_inc(s_landed, 1)

                load(0, 0)
                load(0, 1)
                turns = sp.snap(n[k] // RING)
                with sp.Fori(0, turns - 1) as i:
                    for b in range(2):
                        report(i, b)
                        load(i + 1, b)
                for b in range(2):
                    report(turns - 1, b)
                if name == "pool2":
                    sp.wait_ge(s_tile, tile_mark["top"])
                    sp.dma_start(tables["top"][0:NP, :].rearrange("(t p) w -> p t w", p=P), H[:, :, 0:D]
                                 ).then_inc(s_stored, 16)

        @blk.gpsimd
        def _(pool):
            nc.gpsimd.memset(empty_row[:], 0.0).then_inc(s_dummy, 1)
            pool.wait_ge(s_dummy, 1)
            nc.gpsimd.memset(empty_row[:, HEADS * W_HEAD:], FAR).then_inc(s_dummy, 1)
            pool.wait_ge(s_ready, 1)
            for t in range(NT):
                pool.indirect_dma_start(
                    out=X[:, t, :], out_offset=None, in_=a["x"],
                    in_offset=bass.IndirectOffsetOnAxis(ap=node_i[:, t:t + 1], axis=0),
                    bounds_check=N - 1, oob_is_err=False).then_inc(s_x, 16)
            n = sizes(pool)
            for p, (name, source, k) in enumerate(PHASES):
                base = groups_before(pool, n, p)
                turns_before = pool.snap(base // RING)
                if source != "edges":
                    pool.wait_ge(s_stored, stored_by[source])
                with pool.Fori(0, n[k] // RING) as i:
                    for j in range(RING):
                        b, c = divmod(j * G, BLOCK // 2)
                        if c == 0:
                            hold(pool, s_idx[b], (turns_before + i) * 16 + 16, s_held_pool)
                        hold(pool, s_free, (base + i * RING) + (j + 1), s_held_pool)
                        for g in range(G):
                            if source == "edges":
                                pool.indirect_dma_start(
                                    out=ring_e[:, j, g, :], out_offset=None, in_=a["edge_attr_128"],
                                    in_offset=bass.IndirectOffsetOnAxis(ap=idx[b][:, c + g, 1:2], axis=0),
                                    bounds_check=E - 1, oob_is_err=False).then_inc(s_ring[j], 16)
                            else:
                                w = tables[source].shape[1]
                                pool.indirect_dma_start(
                                    out=ring[:, j, g, 0:w], out_offset=None, in_=tables[source],
                                    in_offset=bass.IndirectOffsetOnAxis(ap=idx[b][:, c + g, 0:1], axis=0),
                                    ).then_inc(s_ring[j], 16)
            if not stop_after:
                pool.wait_ge(s_last, 1)
                for t in range(NT):
                    pool.indirect_dma_start(
                        out=out, out_offset=bass.IndirectOffsetOnAxis(ap=node_i[:, t:t + 1], axis=0),
                        in_=X[:, t, :], in_offset=None, bounds_check=N - 1, oob_is_err=False).then_inc(s_out, 16)
                pool.wait_ge(s_out, 16 * NT)

        @blk.tensor
        def _(pe):
            pe.wait_ge(s_load, 16 * N_LOADS)
            done = 0
            for name, _, _ in PHASES:
                per = len(PRODUCTS[name])
                if per:
                    with pe.Fori(0, NT) as t:
                        for i, mats in enumerate(PRODUCTS[name]):
                            pe.wait_ge(s_in, t * per + (done + i + 1))
                            for j in range(len(mats)):
                                mm = nc.tensor.transpose(ps_tr[:, j, :], ins[:, j, :], ident[:])
                            mm.then_inc(s_tr, 1)
                            pe.wait_ge(s_lhs, t * per + (done + i + 1))
                            for j, m in enumerate(mats):
                                w = MATS[m].shape[1]
                                mm = nc.tensor.matmul(ps_prod[:, 0:w], lhs[:, j, :], MATS[m][:],
                                                      start=(j == 0), stop=(j == len(mats) - 1))
                            mm.then_inc(s_prod, 1)
                    done += per * NT
                if name == "pool2":
                    with pe.Fori(0, SEARCH) as i:
                        pe.wait_ge(s_count, i + 1)
                        nc.tensor.matmul(ps_hits, ones[:], hits[:], start=True, stop=True).then_inc(s_counted, 1)

        @blk.scalar
        def _(act):
            copies, roots, writes = 0, 0, 0
            n = sizes(act)
            for p, (name, _, k) in enumerate(PHASES):
                steps = ACT_STEPS[name]
                nc_, ns_, nw_ = steps.count("c"), steps.count("s"), steps.count("w")
                with act.Fori(0, NT) as t:
                    if name.startswith("att"):
                        base = groups_before(act, n, p, True)
                        mine = act.value_load(groups[0:1, k, bass.ds(t, 1)], min_val=1, max_val=COLS)
                        start = act.value_load(first[0:1, k, bass.ds(t, 1)], min_val=0, max_val=COLS)
                        at = act.snap(base + start)
                        with act.Fori(0, mine) as g:
                            act.wait_ge(s_shift, at + g + 1)
                            nc.scalar.activation(probs[:], shifted[:], ACT.Exp).then_inc(s_probs, 1)
                    ci, si = 0, 0
                    for what in steps:
                        if what == "c":
                            j = len(PRODUCTS[name][ci])
                            ci += 1
                            act.wait_ge(s_tr, t * nc_ + (copies + ci))
                            nc.scalar.copy(lhs[:, 0:j, :], ps_tr[:, 0:j, :]).then_inc(s_lhs, 1)
                        elif what == "s":
                            si += 1
                            act.wait_ge(s_var, t * ns_ + (roots + si))
                            nc.scalar.activation(std[:], mean_var[:, 1:2], ACT.Sqrt, bias=eps[:]).then_inc(s_std, 1)
                        else:
                            table, state, w = STORES[name]
                            act.wait_ge(s_tile, t + (tile_mark[name] + 1))
                            act.dma_start(tables[table][bass.ds(t * P, P), :],
                                          state[:, bass.ds(t, 1), 0:w].rearrange("p a w -> p (a w)")
                                          ).then_inc(s_stored, 16)
                copies, roots, writes = copies + NT * nc_, roots + NT * ns_, writes + NT * nw_
                if name == "pool2":
                    act.wait_ge(s_logit, 1)
                    nc.scalar.activation(col["t0"][:], col["score"][:], ACT.Exp, scale=-1.0).then_inc(s_expd, 1)

        @blk.vector
        def _(dve):
            V = nc.vector
            used = {"in": 0, "var": 0}

            st.by(V.tensor_copy(node_i[:], by_place[:, :, 2]))
            st.by(V.memset(X[:], 0.0))
            st.by(V.memset(eps[:], LN_EPS))
            st.by(V.memset(ring_e[:], 0.0))
            st.by(V.memset(zeros[:], 0.0))
            st.by(V.memset(H[:], 1.0))
            st.settle(dve)
            dve.sem_inc(s_ready, 1)
            dve.sem_inc(s_free, RING)
            din, dout, node = (by_place[:, :, j] for j in range(3))
            st.by(V.tensor_scalar(col["has_in"][:], din, 0.0, None, ALU.is_gt))
            st.by(V.tensor_scalar(col["w_self"][:], din, 0.0, None, ALU.is_equal))
            st.by(V.tensor_scalar(col["t0"][:], din, 1.0, None, ALU.max))
            st.by(V.tensor_scalar(col["real"][:], node, float(N), None, ALU.is_lt))
            st.by(V.tensor_tensor(col["t1"][:], din, dout, ALU.add))
            st.settle(dve)
            st.by(V.reciprocal(col["w_deg"][:], col["t0"][:]))
            st.by(V.tensor_tensor(col["t1"][:], col["t1"][:], col["real"][:], ALU.subtract))
            st.settle(dve)
            st.by(V.tensor_tensor(col["w_mean"][:], col["w_deg"][:], col["has_in"][:], ALU.mult))
            st.by(V.tensor_scalar(col["t1"][:], col["t1"][:], 1.0, None, ALU.add))
            st.settle(dve)
            st.by(V.reciprocal(col["w_count"][:], col["t1"][:]))
            st.settle(dve)
            dve.wait_ge(s_load, 16 * N_LOADS)
            dve.wait_ge(s_x, 16 * NT)

            n = sizes(dve)
            for p, (name, source, k) in enumerate(PHASES):
                att = name.startswith("att")
                dve.wait_ge(s_stored, stored_before[p])
                base = groups_before(dve, n, p)
                mine_before = groups_before(dve, n, p, att)
                per_in, per_var = len(PRODUCTS[name]), ACT_STEPS[name].count("s")
                seen = {"in": 0, "var": 0}
                loop_steps = STEPS[name]
                with dve.Fori(0, NT) as t:
                    st.loop(t, loop_steps)
                    at = bass.ds(t, 1)

                    def tile(state, w=D):
                        return state[:, at, 0:w].rearrange("p a w -> p (a w)")

                    def one(c):
                        return col[c][:, at]

                    def product():
                        seen["in"] += 1
                        st.settle(dve)
                        dve.sem_inc(s_in, 1)
                        hold(dve, s_prod, t * per_in + (used["in"] + seen["in"]), s_held_dve)

                    def norm(dst, src):
                        seen["var"] += 1
                        st.by(V.bn_stats(stats[:], src))
                        st.settle(dve, s_held_dve)
                        st.by(V.bn_aggr(mean_var[:], stats[:]))
                        st.settle(dve)
                        dve.sem_inc(s_var, 1)
                        dve.wait_ge(s_std, t * per_var + (used["var"] + seen["var"]))
                        st.by(V.reciprocal(rstd[:], std[:]))
                        st.settle(dve)
                        st.by(V.tensor_scalar(dst, src, mean_var[:, 0:1], rstd[:], ALU.subtract, ALU.mult))
                        st.settle(dve, s_held_dve)

                    def logits_of(i):
                        feats = H[:, at, 0:HEADS * W_HEAD].rearrange("p a (h c) -> p (a h) c", h=HEADS)[:, :, 0:CH]
                        for j in range(2):
                            st.by(V.tensor_tensor(both[:, j, :].rearrange("p (h c) -> p h c", h=HEADS), feats,
                                                  att_rows[i][:, j, :].rearrange("p (h c) -> p h c", h=HEADS), ALU.mult))
                        st.settle(dve, s_held_dve)
                        st.by(V.tensor_reduce(H[:, at, HEADS * W_HEAD:].rearrange("p a h -> p (a h)"),
                                              both[:, 0, :].rearrange("p (h c) -> p h c", h=HEADS), AX_X, ALU.add))
                        st.by(V.tensor_reduce(to_logit[:, at, :].rearrange("p a h -> p (a h)"),
                                              both[:, 1, :].rearrange("p (h c) -> p h c", h=HEADS), AX_X, ALU.add))

                    def heads(ap):
                        return ap.rearrange("p (h c) -> p h c", h=HEADS)

                    if att:
                        st.by(V.tensor_copy(tile_logit[:], to_logit[:, at, :].rearrange("p a h -> p (a h)")))
                        st.by(V.tensor_copy(att_acc[:], tile(H, HEADS * W_HEAD)))
                        st.by(V.tensor_copy(peak[:], H[:, at, HEADS * W_HEAD:].rearrange("p a h -> p (a h)")))
                        st.settle(dve)
                        st.by(V.tensor_tensor(peak[:], peak[:], tile_logit[:], ALU.add))
                        st.settle(dve)
                        st.by(V.scalar_tensor_tensor(logits[:, G, :], peak[:], 0.2, peak[:], ALU.mult, ALU.max))
                        st.settle(dve)
                    else:
                        st.by(V.memset(acc[:], 0.0))
                        st.settle(dve)

                    mine = dve.value_load(groups[0:1, k, at], min_val=1, max_val=COLS)
                    start = dve.value_load(first[0:1, k, at], min_val=0, max_val=COLS)
                    arrived = dve.snap(base + start)
                    steps_at = dve.snap(mine_before + start)
                    with dve.Fori(0, mine) as g:
                        inner = Count(s_att if att else s_sum)
                        inner.loop(steps_at + g, 7 if att else 2)
                        hold(dve, s_landed, arrived + g + 1, None if att else s_held_dve)
                        entry = bass.ds((arrived + g) & (RING - 1), 1)
                        if att:
                            rows = ring[:, entry, :, :].rearrange("p a g w -> p (a g) w")
                            inner.by(V.tensor_tensor(raw[:], rows[:, :, HEADS * W_HEAD:],
                                                     bc(tile_logit[:], 1, [P, G, HEADS]), ALU.add))
                            inner.settle(dve)
                            inner.by(V.scalar_tensor_tensor(logits[:, 0:G, :], raw[:], 0.2, raw[:], ALU.mult, ALU.max))
                            inner.settle(dve)
                            inner.by(V.tensor_reduce(peak[:], logits[:].rearrange("p g h -> p h g"), AX_X, ALU.max))
                            inner.settle(dve)
                            V.tensor_tensor(shifted[:], logits[:], bc(peak[:], 1, [P, G + 1, HEADS]),
                                            ALU.subtract).then_inc(s_shift, 1)
                            dve.wait_ge(s_probs, steps_at + g + 1)
                            inner.by(V.tensor_copy(logits[:, G, :], peak[:]))
                            inner.by(V.tensor_tensor(
                                weighted[:, 0:G, :].rearrange("p g (h c) -> p g h c", h=HEADS),
                                rows[:, :, 0:HEADS * W_HEAD].rearrange("p g (h c) -> p g h c", h=HEADS),
                                bc(probs[:, 0:G, :], 3, [P, G, HEADS, W_HEAD]), ALU.mult))
                            inner.by(V.tensor_tensor(heads(weighted[:, G, :]), heads(att_acc[:]),
                                                     bc(probs[:, G, :], 2, [P, HEADS, W_HEAD]), ALU.mult))
                            inner.settle(dve)
                            dve.sem_inc(s_free, 1)
                            inner.by(V.tensor_reduce(att_acc[:], weighted[:].rearrange("p g f -> p f g"), AX_X, ALU.add))
                            inner.settle(dve)
                        else:
                            data = ring_e if source == "edges" else ring
                            rows = data[:, entry, :, 0:D].rearrange("p a g w -> p (a g) w")
                            inner.by(V.tensor_reduce(part[:], rows.rearrange("p g w -> p w g"), AX_X, ALU.add))
                            inner.settle(dve, s_held_dve if source == "edges" else None)
                            if source == "edges":
                                V.tensor_copy(rows, bc(zeros[:], 1, [P, G, D])).then_inc(s_free, 1)
                            else:
                                dve.sem_inc(s_free, 1)
                            inner.by(V.tensor_tensor(acc[:], acc[:], part[:], ALU.add))
                            inner.settle(dve)
                        assert inner.k == inner.per, inner.k

                    if name == "mean":
                        st.by(V.tensor_copy(ins[:, 0, :], tile(X)))
                        st.by(V.tensor_scalar(y[:], tile(X), one("w_self"), None, ALU.mult))
                        st.settle(dve)
                        st.by(V.scalar_tensor_tensor(ins[:, 1, :], acc[:], one("w_mean"), y[:], ALU.mult, ALU.add))
                        product()
                        st.by(V.tensor_tensor(y[:], ps_prod[:, 0:D], ROWS["b_mean"][:], ALU.add))
                        st.settle(dve)
                        st.by(V.scalar_tensor_tensor(y[:], y[:], 0.0, tile(X), ALU.max, ALU.add))
                        st.settle(dve)
                        norm(tile(X), y[:])
                        dve.sem_inc(s_tile, 1)
                    elif name.startswith("rel_"):
                        st.by(V.tensor_copy(ins[:, 0, :], acc[:]))
                        product()
                        if name == "rel_nodes_in":
                            st.by(V.tensor_copy(tile(Y), ps_prod[:, 0:D]))
                        else:
                            st.by(V.tensor_tensor(tile(Y), tile(Y), ps_prod[:, 0:D], ALU.add))
                        st.settle(dve)
                        if name == "rel_edges_out":
                            st.by(V.scalar_tensor_tensor(y[:], ROWS["b_fwd"][:], by_place[:, at, 0], tile(Y),
                                                         ALU.mult, ALU.add))
                            st.settle(dve)
                            st.by(V.scalar_tensor_tensor(y[:], ROWS["b_back"][:], by_place[:, at, 1], y[:],
                                                         ALU.mult, ALU.add))
                            st.settle(dve)
                            st.by(V.tensor_scalar(y[:], y[:], one("w_count"), None, ALU.mult))
                            st.settle(dve)
                            st.by(V.scalar_tensor_tensor(y[:], y[:], 0.01, y[:], ALU.mult, ALU.max))
                            st.settle(dve)
                            st.by(V.tensor_tensor(y[:], y[:], tile(X), ALU.add))
                            st.settle(dve)
                            norm(z[:], y[:])
                            st.by(V.tensor_tensor(z[:], z[:], ROWS["gamma"][:], ALU.mult))
                            st.settle(dve)
                            st.by(V.tensor_tensor(z[:], z[:], ROWS["beta"][:], ALU.add))
                            st.settle(dve)
                            st.by(V.tensor_tensor(y[:], z[:], tile(X), ALU.add))
                            st.settle(dve)
                            norm(tile(X), y[:])
                            st.by(V.tensor_copy(ins[:, 0, :], tile(X)))
                            product()
                            st.by(V.tensor_copy(heads(tile(H, HEADS * W_HEAD))[:, :, 0:CH], heads(ps_prod[:, 0:D])))
                            st.by(V.tensor_tensor(y[:], ps_prod[:, D:2 * D], tile(X), ALU.add))
                            st.settle(dve)
                            st.by(V.tensor_tensor(y[:], y[:], ROWS["b_res"][:], ALU.add))
                            st.settle(dve)
                            st.by(V.tensor_tensor(tile(Y), y[:], ROWS["b_att2"][:], ALU.add))
                            logits_of(0)
                            st.settle(dve)
                            dve.sem_inc(s_tile, 1)
                    elif att:
                        st.by(V.reciprocal(r_sum[:], heads(att_acc[:])[:, :, CH]))
                        st.settle(dve)
                        st.by(V.tensor_tensor(heads(y[:]), heads(att_acc[:])[:, :, 0:CH],
                                              bc(r_sum[:], 2, [P, HEADS, CH]), ALU.mult))
                        st.settle(dve)
                        if name == "att1":
                            st.by(V.tensor_tensor(y[:], y[:], ROWS["b_att1"][:], ALU.add))
                            st.settle(dve)
                            st.by(V.tensor_scalar(ins[:, 0, :], y[:], 0.0, None, ALU.max))
                            product()
                            st.by(V.tensor_copy(heads(tile(H, HEADS * W_HEAD))[:, :, 0:CH], heads(ps_prod[:, 0:D])))
                            st.settle(dve)
                            logits_of(1)
                            st.settle(dve)
                        else:
                            st.by(V.tensor_tensor(y[:], y[:], tile(Y), ALU.add))
                            st.settle(dve)
                            norm(tile(X), y[:])
                        dve.sem_inc(s_tile, 1)
                    else:
                        state = {"pool1": X, "pool2": H, "pool3": H, "pool4": Y}[name]
                        st.by(V.tensor_copy(ins[:, 0, :], tile(state)))
                        st.by(V.tensor_scalar(ins[:, 1, :], acc[:], one("w_deg"), None, ALU.mult))
                        product()
                        bias = ROWS[{"pool1": "b_s1", "pool2": "b_s2", "pool3": "b_us1", "pool4": "b_us2"}[name]]
                        st.by(V.tensor_tensor(y[:], ps_prod[:, 0:D], bias[:], ALU.add))
                        st.settle(dve)
                        if name in ("pool1", "pool3"):
                            st.by(V.tensor_scalar(tile(H if name == "pool1" else Y), y[:], 0.0, None, ALU.max))
                            st.settle(dve)
                            dve.sem_inc(s_tile, 1)
                        elif name == "pool2":
                            st.by(V.tensor_tensor(z[:], y[:], ROWS["w_score"][:], ALU.mult))
                            st.by(V.tensor_copy(tile(Y), y[:]))
                            st.settle(dve, s_held_dve)
                            st.by(V.tensor_reduce(one("score"), z[:], AX_X, ALU.add))
                            st.settle(dve)
                        else:
                            st.by(V.tensor_tensor(y[:], y[:], tile(X), ALU.add))
                            st.settle(dve)
                            norm(tile(X), y[:])
                used["in"] += NT * per_in
                used["var"] += NT * per_var
                st.end(NT)

                if name == "pool2":
                    score, chosen, t0, t1 = (col[c][:] for c in ("score", "chosen", "t0", "t1"))
                    st.by(V.tensor_scalar(score, score, b_score[:], None, ALU.add))
                    st.settle(dve)
                    dve.sem_inc(s_logit, 1)
                    dve.wait_ge(s_expd, 1)
                    st.by(V.tensor_scalar(t0, t0, 1.0, None, ALU.add))
                    st.settle(dve)
                    st.by(V.reciprocal(t1, t0))
                    st.settle(dve)
                    st.by(V.tensor_tensor(t0, t1, col["real"][:], ALU.mult))
                    st.by(V.tensor_scalar(score, col["real"][:], -1.0, None, ALU.add))
                    st.settle(dve)
                    st.by(V.tensor_tensor(score, score, t0, ALU.add))
                    st.by(V.memset(thr[:], 0))
                    st.by(V.memset(bit[:], 1 << SCORE_BITS))
                    st.settle(dve)

                    def search(trips, offset, count_hits, limit, op):
                        with dve.Fori(0, trips) as i:
                            st.loop(i, 7 if trips == SCORE_BITS else 9)
                            st.by(V.tensor_scalar(bit[:], bit[:], 1, None, ALU.logical_shift_right))
                            st.settle(dve)
                            st.by(V.tensor_tensor(cand[:], thr[:], bit[:], ALU.bitwise_or))
                            st.settle(dve)
                            count_hits()
                            st.by(V.tensor_reduce(hits[:], t0, AX_X, ALU.add))
                            st.settle(dve)
                            dve.sem_inc(s_count, 1)
                            dve.wait_ge(s_counted, i + (offset + 1))
                            st.by(V.tensor_scalar(keep[:], ps_hits, limit, -1.0, op, ALU.mult))
                            st.settle(dve)
                            st.by(V.tensor_tensor(keep[:], keep[:], bit[:], ALU.bitwise_and))
                            st.settle(dve)
                            st.by(V.tensor_tensor(thr[:], thr[:], keep[:], ALU.bitwise_or))
                            st.settle(dve)
                        st.end(trips)

                    def above():
                        st.by(V.tensor_scalar(t0, score, cand[:].bitcast(F32), None, ALU.is_ge))
                        st.settle(dve)

                    def ties_before():
                        st.by(V.tensor_copy(cand_f[:], cand[:]))
                        st.settle(dve)
                        st.by(V.tensor_scalar(t0, node, cand_f[:], None, ALU.is_lt))
                        st.settle(dve)
                        st.by(V.tensor_tensor(t0, t0, t1, ALU.mult))
                        st.settle(dve)

                    search(SCORE_BITS, 0, above, float(TOP), ALU.is_ge)
                    st.by(V.tensor_scalar(chosen, score, thr[:].bitcast(F32), None, ALU.is_gt))
                    st.by(V.tensor_scalar(t1, score, thr[:].bitcast(F32), None, ALU.is_equal))
                    st.settle(dve)
                    st.by(V.tensor_reduce(hits[:], chosen, AX_X, ALU.add))
                    st.by(V.memset(thr[:], 0))
                    st.by(V.memset(bit[:], 1 << NODE_BITS))
                    st.settle(dve)
                    dve.sem_inc(s_count, 1)
                    dve.wait_ge(s_counted, SCORE_BITS + 1)
                    st.by(V.tensor_scalar(need[:], ps_hits, -1.0, float(TOP), ALU.mult, ALU.add))
                    st.settle(dve)
                    search(NODE_BITS, SCORE_BITS + 1, ties_before, need[:], ALU.is_le)
                    st.by(V.tensor_copy(cand_f[:], thr[:]))
                    st.settle(dve)
                    st.by(V.tensor_scalar(t0, node, cand_f[:], None, ALU.is_lt))
                    st.settle(dve)
                    st.by(V.tensor_tensor(t0, t0, t1, ALU.mult))
                    st.settle(dve)
                    st.by(V.tensor_tensor(chosen, chosen, t0, ALU.add))
                    st.settle(dve)
                    st.by(V.tensor_tensor(H[:, :, 0:D], Y[:], bc(chosen, 2, [P, NT, D]), ALU.mult))
                    st.settle(dve)
                    dve.sem_inc(s_tile, 1)
            dve.sem_inc(s_last, 1)


_OUTS = [((6250, 128), "float32")]


def laid_out(inputs):
    arrays = {n: v for n, v in inputs.items() if n not in ("L1_gnn_queries",)}
    for new, old in (("W0T", "L0_gnn_W"), ("WfT", "L1_gnn_W_fwd"), ("WbT", "L1_gnn_W_back")):
        arrays[new] = arrays.pop(old).T
    return arrays


def kernel(**inputs):
    import numpy as _np
    import concourse.bacc as _bacc
    from concourse import mybir as _mybir
    from concourse.bass_utils import run_bass_kernel_spmd as _run

    nc = _bacc.Bacc("TRN2", target_bir_lowering=False, num_devices=1)
    arrays, args = {}, {}
    for name, v in laid_out(inputs).items():
        v = _np.ascontiguousarray(v)
        arrays[name] = v
        args[name] = nc.dram_tensor(name, v.shape, _mybir.dt.from_np(v.dtype), kind="ExternalInput").ap()
    (shape, dtype), = _OUTS
    out = nc.dram_tensor("out_x", shape, _mybir.dt.from_np(_np.dtype(dtype)), kind="ExternalOutput").ap()
    gnn_kernel(nc, args, out)
    r = _run(nc, [arrays], core_ids=[0])
    return r.results[0]["out_x"]
```

```python
from contextlib import ExitStack

import concourse.bass as bass
from concourse import mybir

ALU = mybir.AluOpType
ACT = mybir.ActivationFunctionType
F32 = mybir.dt.float32
BF16 = mybir.dt.bfloat16
I32 = mybir.dt.int32
I16 = mybir.dt.int16
AX_X = mybir.AxisListType.X
RMAX = bass.bass_isa.ReduceOp.max

P = 128
G = 4
RING = 8
BLOCK = RING * G
QUAD = 4
SEVEN = 7
HB = 16
FILL = 512
PIECES = 3
LN_EPS = 1e-5
BY_DST, BY_SRC, REST = 0, 1, 2
FAR = -1e30


class Count:

    def __init__(self, sem):
        self.sem, self.base, self.k, self.at, self.per = sem, 0, 0, None, 0

    def loop(self, at, per_turn):
        self.base += self.k
        self.at, self.k, self.per = at, 0, per_turn

    def end(self, trips):
        assert self.k == self.per, (self.k, self.per)
        self.base += trips * self.per
        self.at, self.k = None, 0

    def by(self, ins, n=1):
        self.k += n
        return ins.then_inc(self.sem, n)

    def settle(self, eng, alone=None):
        v = self.base + self.k
        hold(eng, self.sem, v if self.at is None else self.at * self.per + v, alone)


def hold(eng, sem, value, alone):
    eng.wait_ge(sem, value)
    if alone is not None:
        eng.sem_inc(alone, 1)


def bc(ap, axis, shape):
    return ap.unsqueeze(axis).broadcast_to(shape)


def gnn_kernel(nc, a, out, stop_after=None):
    N, D = a["x"].shape
    E = a["src"].shape[0]
    NT = -(-N // (P * SEVEN)) * SEVEN
    NP = NT * P
    HI = NT + 1
    BODY = 2 * QUAD
    TC = -(-E // (P * HB)) * HB
    FULL, OVER = divmod(E, TC)
    COLS = -(-(E + NT * G + 2 * BLOCK) // FILL) * FILL + FILL
    DUMMY_NODE, DUMMY_EDGE = NP, E
    ND = PIECES * SEVEN
    WP = SEVEN * P
    BANK = 512
    EDGE_COPY = E // 10
    EXACT = 256
    HEADS, CH = a["L2_gnn_a1_src"].shape
    TOP = max(1, N // 4)
    H_TURNS, J_TURNS, R_TURNS = TC // HB, TC // BODY, NT // SEVEN
    assert D == P and HEADS * CH == D and P * COLS + P * HB < 1 << 24 and NT == ND + 4 * SEVEN and E % EDGE_COPY == 0

    with ExitStack() as ctx:
        def sb(name, shape, dt=F32):
            return ctx.enter_context(nc.sbuf_tensor(name, shape, dt))

        def psum(name, shape, dt=F32):
            return ctx.enter_context(nc.psum_tensor(name, shape, dt))

        def sem(name):
            return ctx.enter_context(nc.semaphore(name))

        def dram(name, shape, dt=F32):
            return nc.dram_tensor(name, shape, dt).ap()

        slots = [dram(f"slots_{k}", (P * COLS + P * HB, 2), I32) for k in ("by_dst", "by_src")]
        nodes_by_place = dram("nodes_by_place", (NP, 4))
        edge_rows = dram("edge_rows", (E + 1, D))

        iota_b = sb("iota_b", [P, P], BF16)
        iota_f = sb("iota_f", [P, P])
        part_f = sb("part_f", [P, 1])
        earlier = sb("earlier", [P, P], BF16)
        earlier_f = sb("earlier_f", [P, P])
        ident_b = sb("ident_b", [P, P], BF16)
        ident = sb("ident", [P, P])
        ones_b = sb("ones_b", [P, 1], BF16)
        ones = sb("ones", [P, P])
        zeros_b = sb("zeros_b", [P, P], BF16)

        bank = [psum(f"bank{i}", [P, 512]) for i in range(8)]

        s_const = sem("s_const")
        s_dve = sem("s_dve")
        s_meta = sem("s_meta")
        s_binned = sem("s_binned")
        s_held_dve = sem("s_held_dve")
        s_held_pool = sem("s_held_pool")
        s_edges = sem("s_edges")

        groups = sb("groups", [P, 3, NT], I32)
        first = sb("first", [P, 3, NT], I32)
        total = sb("total", [P, 3, 2], I32)
        large = sb("large", [P, 1], I32)
        by_place = sb("by_place", [P, NT, 4])
        st = Count(s_dve)

        with ExitStack() as binning:
            def sbb(name, shape, dt=F32):
                return binning.enter_context(nc.sbuf_tensor(name, shape, dt))

            def bsem(name):
                return binning.enter_context(nc.semaphore(name))

            ends = sbb("ends", [P, 2, TC], I32)
            scratch = sbb("scratch", [P, 2, TC], I32)
            lo = sbb("lo", [P, 2, TC], BF16)
            hi = sbb("hi", [P, 2, TC], BF16)
            edge_no = sbb("edge_no", [P, TC], I32)
            is_lo = [sbb(f"is_lo{k}", [P, HB, P], BF16) for k in range(2)]
            is_hi = [sbb(f"is_hi{k}", [P, HB, HI], BF16) for k in range(2)]
            degree = sbb("degree", [P, 2, HI])
            node_rows = sbb("node_rows", [P, NT, 4])
            bin_f = sbb("bin_f", [P, NT])
            is_bin = sbb("is_bin", [P, SEVEN, P], BF16)
            bin_T = sbb("bin_T", [P, SEVEN, P], BF16)
            bin_Tf = sbb("bin_Tf", [P, SEVEN, P])
            bin_same = sbb("bin_same", [P, SEVEN, P], BF16)
            bin_count = [sbb(f"bin_count{i}", [P, NT + 1]) for i in range(2)]
            bin_base = sbb("bin_base", [P, SEVEN])
            place_f = sbb("place_f", [P, NT])
            place_i = sbb("place_i", [P, NT], I32)
            place_x = sbb("place_x", [P, NT], I32)
            place_part = sbb("place_part", [P, NT])
            place_tile = sbb("place_tile", [P, NT])
            tile_pick = sbb("tile_pick", [P, NT, NT])
            most = sbb("most", [P, 2, NT])
            most_all = sbb("most_all", [P, 2, NT])
            most_out = sbb("most_out", [P, 1])
            count_f = sbb("count_f", [P, 2, NT])
            scan = [sbb(f"scan{i}", [P, 2, NT + 1]) for i in range(2)]
            tot_i = sbb("tot_i", [P, 3, 2], I32)
            first_f = sbb("first_f", [P, NT + 1])
            running = sbb("running", [P, 2, 2, HI])
            fill = sbb("fill", [P, FILL, 2], I32)
            q_lo = [[sbb(f"q_lo{b}{k}", [P, QUAD, P], BF16) for k in range(2)] for b in range(2)]
            q_hi = [[sbb(f"q_hi{b}{k}", [P, QUAD, HI], BF16) for k in range(2)] for b in range(2)]
            lo_T = [[sbb(f"lo_T{b}{k}", [P, QUAD, P], BF16) for k in range(2)] for b in range(2)]
            lo_Tf = [[sbb(f"lo_Tf{b}{k}", [P, QUAD, P]) for k in range(2)] for b in range(2)]
            same = [sbb(f"same{k}", [P, QUAD, P], BF16) for k in range(2)]
            picked = sbb("picked", [P, 2, QUAD, 2, HI])
            found = sbb("found", [P, 2, QUAD, 2])
            slot_no = [sbb(f"slot_no{b}", [P, 2, QUAD], I32) for b in range(2)]
            record = [sbb(f"record{b}", [P, 2, QUAD, 2], I32) for b in range(2)]

            s_ends = bsem("s_ends")
            s_onehot = bsem("s_onehot")
            s_hist = bsem("s_hist")
            s_bins = bsem("s_bins")
            s_binsum = bsem("s_binsum")
            s_binsum_read = bsem("s_binsum_read")
            s_bincol = bsem("s_bincol")
            s_binT = bsem("s_binT")
            s_binTc = bsem("s_binTc")
            s_binE = bsem("s_binE")
            s_binM = bsem("s_binM")
            s_rank = bsem("s_rank")
            s_places = bsem("s_places")
            s_rows_out = bsem("s_rows_out")
            s_rows_in = bsem("s_rows_in")
            s_most = bsem("s_most")
            s_most_all = bsem("s_most_all")
            s_filled = bsem("s_filled")
            s_fill_done = bsem("s_fill_done")
            s_quad = [bsem(f"s_quad{k}") for k in range(2)]
            s_T = [bsem(f"s_T{k}") for k in range(2)]
            s_Tcopy = [bsem(f"s_Tcopy{k}") for k in range(2)]
            s_same = [bsem(f"s_same{k}") for k in range(2)]
            s_mask = [bsem(f"s_mask{k}") for k in range(2)]
            s_run = [bsem(f"s_run{k}") for k in range(2)]
            s_runcopy = [bsem(f"s_runcopy{k}") for k in range(2)]
            s_found = [bsem(f"s_found{k}") for k in range(2)]
            s_taken = [bsem(f"s_taken{k}") for k in range(2)]
            s_record = bsem("s_record")
            s_record_free = bsem("s_record_free")
            s_scatter = [bsem(f"s_scatter{b}") for b in range(2)]

            ps_hist = [bank[k][:, 0:HI] for k in range(2)]
            ps_count = bank[2][:, 0:SEVEN]
            ps_start = bank[3][:, 0:1]
            ps_binT = bank[4][:].bitcast(BF16)[:, 0:SEVEN * P].rearrange("p (c f) -> p c f", c=SEVEN)
            ps_binE = [bank[5][:].rearrange("p (c f) -> p c f", c=4), bank[6][:].rearrange("p (c f) -> p c f", c=4)]
            ps_rank = bank[7][:, 0:SEVEN]
            ps_T = [bank[k][:].bitcast(BF16)[:, 0:QUAD * P].rearrange("p (c f) -> p c f", c=QUAD) for k in range(2)]
            ps_same = [bank[2 + k][:].rearrange("p (c f) -> p c f", c=QUAD) for k in range(2)]
            ps_found = [bank[4 + k][:, 0:QUAD * 2 * HI].rearrange("p (c f) -> p c f", c=QUAD) for k in range(2)]
            ps_run = [bank[6 + k][:, 0:HI] for k in range(2)]

            blk = binning.enter_context(nc.Block())

            @blk.sync
            def _(sp):
                sp.wait_ge(s_const, 1)
                for k, name in ((BY_DST, "dst"), (BY_SRC, "src")):
                    sp.dma_start(ends[0:FULL, k, :], a[name][0:FULL * TC].rearrange("(p c) -> p c", c=TC)
                                 ).then_inc(s_ends, 16)
                    sp.dma_start(ends[FULL:FULL + 1, k, 0:OVER],
                                 a[name][FULL * TC:E].rearrange("(p c) -> p c", p=1)).then_inc(s_ends, 16)
                sp.wait_ge(s_rows_out, 16 * NT)
                sp.dma_start(by_place[:], nodes_by_place.rearrange("(t p) w -> p t w", p=P)).then_inc(s_rows_in, 16)
                sp.wait_ge(s_meta, 1)
                fills = [sp.value_load(total[0:1, k, 1:2], min_val=1, max_val=COLS // FILL) for k in range(2)]
                for k in range(2):
                    table = slots[k][0:P * COLS, :].rearrange("(p c) w -> p c w", p=P)
                    with sp.Fori(0, fills[k]) as i:
                        sp.dma_start(table[:, bass.ds(i * FILL, FILL), :], fill[:]).then_inc(s_filled, 16)
                sp.wait_ge(s_filled, (fills[0] + fills[1]) * 16)
                sp.sem_inc(s_fill_done, 1)
                sp.sem_inc(s_record_free, 2)
                with sp.Fori(0, J_TURNS) as i:
                    for b in range(2):
                        sp.wait_ge(s_scatter[b], i * (16 * 2 * QUAD) + 16 * 2 * QUAD)
                        sp.sem_inc(s_record_free, 1)

            @blk.gpsimd
            def _(pool):
                nc.gpsimd.memset(ends[:], NT * P).then_inc(s_const, 1)
                nc.gpsimd.memset(ones[:], 1.0).then_inc(s_const, 1)
                nc.gpsimd.iota(iota_b[:], [[1, P]], base=0, channel_multiplier=0,
                               allow_small_or_imprecise_dtypes=True)
                nc.gpsimd.iota(iota_f[:], [[1, P]], base=0, channel_multiplier=0,
                               allow_small_or_imprecise_dtypes=True)
                nc.gpsimd.iota(part_f[:], [[0, 1]], base=0, channel_multiplier=1,
                               allow_small_or_imprecise_dtypes=True)
                nc.gpsimd.iota(edge_no[:], [[1, TC]], base=0, channel_multiplier=TC)
                nc.gpsimd.iota(node_rows[:, :, 2:4], [[P, NT], [0, 2]], base=0, channel_multiplier=1,
                               allow_small_or_imprecise_dtypes=True)
                nc.gpsimd.memset(ones_b[:], 1.0)
                nc.gpsimd.memset(zeros_b[:], 0.0)
                nc.gpsimd.memset(fill[:, :, 0:1], DUMMY_NODE)
                nc.gpsimd.memset(fill[:, :, 1:2], DUMMY_EDGE)
                pool.wait_ge(s_const, 2)
                for m, op in ((earlier, ALU.is_gt), (earlier_f, ALU.is_gt), (ident_b, ALU.is_equal),
                              (ident, ALU.is_equal)):
                    last = nc.gpsimd.affine_select(out=m[:], in_=ones[:], compare_op=op, fill=0.0, base=0,
                                                   pattern=[[1, P]], channel_multiplier=-1)
                last.then_inc(s_const, 1)
                pool.wait_ge(s_places, 1)
                for t in range(NT):
                    pool.indirect_dma_start(
                        out=nodes_by_place, out_offset=bass.IndirectOffsetOnAxis(ap=place_i[:, t:t + 1], axis=0),
                        in_=node_rows[:, t, :], in_offset=None).then_inc(s_rows_out, 16)
                pool.wait_ge(s_most, 1)
                nc.gpsimd.partition_all_reduce(most_all[:].rearrange("p a b -> p (a b)"),
                                               most[:].rearrange("p a b -> p (a b)"), P, RMAX).then_inc(s_most_all, 1)
                pool.wait_ge(s_fill_done, 1)
                with pool.Fori(0, J_TURNS) as i:
                    for b in range(2):
                        hold(pool, s_record, i * 2 + (b + 1), s_held_pool)
                        for k in range(2):
                            for q in range(QUAD):
                                pool.indirect_dma_start(
                                    out=slots[k],
                                    out_offset=bass.IndirectOffsetOnAxis(ap=slot_no[b][:, k, q:q + 1], axis=0),
                                    in_=record[b][:, k, q, :], in_offset=None).then_inc(s_scatter[b], 16)
                for b in range(2):
                    pool.wait_ge(s_scatter[b], 16 * 2 * QUAD * J_TURNS)
                pool.sem_inc(s_binned, 1)

            @blk.tensor
            def _(pe):
                pe.wait_ge(s_const, 3)
                for k in range(2):
                    nc.tensor.matmul(ps_hist[k], zeros_b[:], zeros_b[:, 0:HI], start=True, stop=False,
                                     skip_group_check=True)
                pe.sem_inc(s_hist, 2)
                with pe.Fori(0, H_TURNS) as i:
                    for k in range(2):
                        pe.wait_ge(s_onehot, i * 2 + (k + 1))
                        for c in range(HB):
                            mm = nc.tensor.matmul(ps_hist[k], is_lo[k][:, c, :], is_hi[k][:, c, :],
                                                  start=False, stop=False, skip_group_check=True)
                        mm.then_inc(s_hist, 1)
                pe.sem_inc(s_binsum, 1)
                with pe.Fori(0, R_TURNS) as i:
                    pe.wait_ge(s_bins, i + 1)
                    pe.wait_ge(s_binsum_read, i + 1)
                    for c in range(SEVEN):
                        mm = nc.tensor.matmul(ps_count[:, c:c + 1], is_bin[:, c, :], ones_b[:], start=True, stop=True)
                    mm.then_inc(s_binsum, 1)
                pe.wait_ge(s_bincol, 1)
                nc.tensor.matmul(ps_start, earlier_f[:], bin_count[0][:, NT:NT + 1], start=True,
                                 stop=True).then_inc(s_binsum, 1)
                pe.sem_inc(s_rank, 1)
                with pe.Fori(0, R_TURNS) as i:
                    pe.wait_ge(s_bins, i + (R_TURNS + 1))
                    for c in range(SEVEN):
                        mm = nc.tensor.transpose(ps_binT[:, c, :], is_bin[:, c, :], ident_b[:])
                    mm.then_inc(s_binT, 1)
                    pe.wait_ge(s_binTc, i + 1)
                    for c in range(SEVEN):
                        mm = nc.tensor.matmul(ps_binE[c // 4][:, c % 4, :], bin_T[:, c, :], bin_T[:, c, :],
                                              start=True, stop=True)
                    mm.then_inc(s_binE, 1)
                    pe.wait_ge(s_binM, i + 1)
                    for c in range(SEVEN):
                        nc.tensor.matmul(ps_rank[:, c:c + 1], bin_Tf[:, c, :], bin_base[:, c:c + 1],
                                         start=True, stop=False)
                        mm = nc.tensor.matmul(ps_rank[:, c:c + 1], bin_same[:, c, :], ones_b[:],
                                              start=False, stop=True)
                    mm.then_inc(s_rank, 1)
                pe.wait_ge(s_meta, 2)
                for k in range(2):
                    nc.tensor.matmul(ps_run[k], ident[:], running[:, k, 0, :], start=True, stop=False,
                                     skip_group_check=True)
                    pe.sem_inc(s_run[k], 2 * QUAD)
                with pe.Fori(0, J_TURNS) as i:
                    for b in range(2):
                        for k in range(2):
                            pe.wait_ge(s_quad[k], i * 2 + (b + 1))
                            pe.wait_ge(s_Tcopy[k], i * 2 + (b + 1))
                            for c in range(QUAD):
                                mm = nc.tensor.transpose(ps_T[k][:, c, :], q_lo[b][k][:, c, :], ident_b[:])
                            mm.then_inc(s_T[k], 1)
                    for b in range(2):
                        for k in range(2):
                            pe.wait_ge(s_Tcopy[k], i * 2 + (b + 2))
                            pe.wait_ge(s_mask[k], i * 2 + (b + 1))
                            for c in range(QUAD):
                                mm = nc.tensor.matmul(ps_same[k][:, c, :], lo_T[b][k][:, c, :], lo_T[b][k][:, c, :],
                                                      start=True, stop=True)
                            mm.then_inc(s_same[k], 1)
                        for k in range(2):
                            pe.wait_ge(s_mask[k], i * 2 + (b + 2))
                            pe.wait_ge(s_taken[k], i * 2 + (b + 1))
                        for c in range(QUAD):
                            for k in range(2):
                                pe.wait_ge(s_runcopy[k], i * (2 * QUAD) + (b * QUAD + c + 1))
                                nc.tensor.matmul(ps_found[k][:, c, :], lo_Tf[b][k][:, c, :],
                                                 running[:, k, :, :].rearrange("p a b -> p (a b)"),
                                                 start=True, stop=False, skip_group_check=True)
                                mm = nc.tensor.matmul(ps_found[k][:, c, 0:HI], same[k][:, c, :], q_hi[b][k][:, c, :],
                                                      start=False, stop=True, skip_group_check=True)
                                if c == QUAD - 1:
                                    mm.then_inc(s_found[k], 1)
                                nc.tensor.matmul(ps_run[k], q_lo[b][k][:, c, :], q_hi[b][k][:, c, :],
                                                 start=False, stop=False, skip_group_check=True).then_inc(s_run[k], 1)

            @blk.scalar
            def _(act):
                for c in range(0, E, EDGE_COPY):
                    act.dma_start(edge_rows[c:c + EDGE_COPY, :],
                                  a["edge_attr_128"][c:c + EDGE_COPY, :]).then_inc(s_edges, 16)
                with act.Fori(0, R_TURNS) as i:
                    act.wait_ge(s_binT, i + 1)
                    act.wait_ge(s_rank, i + 1)
                    nc.scalar.copy(bin_T[:], ps_binT)
                    nc.scalar.copy(bin_Tf[:], ps_binT).then_inc(s_binTc, 1)
                for k in range(2):
                    act.sem_inc(s_Tcopy[k], 1)
                    act.sem_inc(s_runcopy[k], 1)
                with act.Fori(0, J_TURNS) as i:
                    for b in range(2):
                        for k in range(2):
                            act.wait_ge(s_T[k], i * 2 + (b + 1))
                            act.wait_ge(s_run[k], i * (2 * QUAD) + QUAD * (b + 1))
                            nc.scalar.copy(lo_T[b][k][:], ps_T[k])
                            nc.scalar.copy(lo_Tf[b][k][:], ps_T[k]).then_inc(s_Tcopy[k], 1)
                    for b in range(2):
                        for c in range(QUAD):
                            for k in range(2):
                                act.wait_ge(s_run[k], i * (2 * QUAD) + (2 * QUAD + b * QUAD + c + 1))
                                nc.scalar.copy(running[:, k, 0, :], ps_run[k]).then_inc(s_runcopy[k], 1)

            @blk.vector
            def _(dve):
                V = nc.vector
                dve.wait_ge(s_const, 3)
                dve.wait_ge(s_ends, 64)
                st.by(V.tensor_scalar(scratch[:], ends[:], P - 1, None, ALU.bitwise_and))
                st.settle(dve)
                st.by(V.tensor_copy(lo[:], scratch[:]))
                st.settle(dve)
                st.by(V.tensor_scalar(scratch[:], ends[:], 7, None, ALU.logical_shift_right))
                st.settle(dve)
                st.by(V.tensor_copy(hi[:], scratch[:]))
                st.settle(dve)

                with dve.Fori(0, H_TURNS) as i:
                    for k in range(2):
                        dve.wait_ge(s_hist, i * 2 + (k + 1))
                        V.tensor_tensor(is_lo[k][:], bc(lo[:, k, bass.ds(i * HB, HB)], 2, [P, HB, P]),
                                        bc(iota_b[:], 1, [P, HB, P]), ALU.is_equal)
                        V.tensor_tensor(is_hi[k][:], bc(hi[:, k, bass.ds(i * HB, HB)], 2, [P, HB, HI]),
                                        bc(iota_b[:, 0:HI], 1, [P, HB, HI]), ALU.is_equal).then_inc(s_onehot, 1)
                dve.wait_ge(s_hist, 2 * H_TURNS + 2)
                for k in range(2):
                    st.by(V.tensor_copy(degree[:, k, :], ps_hist[k]))
                st.settle(dve)
                st.by(V.tensor_tensor(bin_f[:], degree[:, 0, 0:NT], degree[:, 1, 0:NT], ALU.add))
                for k in range(2):
                    st.by(V.tensor_copy(node_rows[:, :, k], degree[:, k, 0:NT]))
                st.settle(dve)
                st.by(V.tensor_scalar(bin_f[:], bin_f[:], float(P - 1), -1.0, ALU.min, ALU.mult))
                st.settle(dve)
                st.by(V.tensor_scalar(bin_f[:], bin_f[:], float(P - 1), None, ALU.add))
                st.settle(dve)

                def bins(i, waits):
                    for s, v in waits:
                        dve.wait_ge(s, v)
                    V.tensor_tensor(is_bin[:], bc(bin_f[:, bass.ds(i * SEVEN, SEVEN)], 2, [P, SEVEN, P]),
                                    bc(iota_f[:], 1, [P, SEVEN, P]), ALU.is_equal).then_inc(s_bins, 1)

                dve.sem_inc(s_binsum_read, 1)
                with dve.Fori(0, R_TURNS) as i:
                    bins(i, [(s_binsum, i + 1)])
                    hold(dve, s_binsum, i + 2, s_held_dve)
                    V.tensor_copy(bin_count[1][:, bass.ds(i * SEVEN + 1, SEVEN)], ps_count).then_inc(s_binsum_read, 1)
                st.by(V.memset(bin_count[1][:, 0:1], 0.0))
                dve.wait_ge(s_binsum_read, R_TURNS + 1)
                st.settle(dve)
                now, step = 1, 1
                while step < NT + 1:
                    src, dst = bin_count[now], bin_count[1 - now]
                    st.by(V.tensor_copy(dst[:, 0:step], src[:, 0:step]))
                    st.by(V.tensor_tensor(dst[:, step:], src[:, step:], src[:, 0:NT + 1 - step], ALU.add))
                    st.settle(dve)
                    now, step = 1 - now, 2 * step
                if now == 1:
                    st.by(V.tensor_copy(bin_count[0][:], bin_count[1][:]))
                    st.settle(dve)
                dve.sem_inc(s_bincol, 1)
                dve.wait_ge(s_binsum, R_TURNS + 2)
                st.by(V.tensor_copy(bin_base[:, 0:1], ps_start))
                st.settle(dve)
                st.by(V.tensor_scalar(bin_count[1][:], bin_count[0][:], bin_base[:, 0:1], None, ALU.add))
                st.settle(dve)
                with dve.Fori(0, R_TURNS) as i:
                    bins(i, [(s_rank, i + 1)])
                    V.tensor_copy(bin_base[:], bin_count[1][:, bass.ds(i * SEVEN, SEVEN)])
                    dve.wait_ge(s_binE, i + 1)
                    V.tensor_tensor(bin_same[:, 0:4, :], ps_binE[0], bc(earlier_f[:], 1, [P, 4, P]), ALU.mult)
                    V.tensor_tensor(bin_same[:, 4:SEVEN, :], ps_binE[1][:, 0:SEVEN - 4, :],
                                    bc(earlier_f[:], 1, [P, SEVEN - 4, P]), ALU.mult).then_inc(s_binM, 1)
                    hold(dve, s_rank, i + 2, s_held_dve)
                    V.tensor_copy(place_f[:, bass.ds(i * SEVEN, SEVEN)], ps_rank).then_inc(s_binsum_read, 1)
                dve.wait_ge(s_binsum_read, 2 * R_TURNS + 1)
                V.tensor_copy(place_i[:], place_f[:]).then_inc(s_places, 1)
                dve.wait_ge(s_places, 1)
                st.by(V.tensor_scalar(place_x[:], place_i[:], P - 1, None, ALU.bitwise_and))
                st.settle(dve)
                st.by(V.tensor_copy(place_part[:], place_x[:]))
                st.settle(dve)
                st.by(V.tensor_scalar(place_x[:], place_i[:], 7, None, ALU.logical_shift_right))
                st.settle(dve)
                st.by(V.tensor_copy(place_tile[:], place_x[:]))
                st.settle(dve)
                dve.wait_ge(s_rows_in, 16)
                V.tensor_copy(most[:].rearrange("p k t -> p t k"), by_place[:, :, 0:2]).then_inc(s_most, 1)
                dve.wait_ge(s_most_all, 1)
                st.by(V.tensor_scalar(groups[:, 0:2, :], most_all[:], float(G - 1), None, ALU.add))
                st.by(V.tensor_reduce(most_out[:], most_all[:, BY_SRC, :], AX_X, ALU.max))
                st.settle(dve)
                st.by(V.tensor_scalar(groups[:, 0:2, :], groups[:, 0:2, :], 2, None, ALU.logical_shift_right))
                st.by(V.tensor_scalar(large[:], most_out[:], float(EXACT), None, ALU.is_gt))
                st.settle(dve)
                st.by(V.tensor_scalar(groups[:, 0:2, :], groups[:, 0:2, :], 1, None, ALU.max))
                st.settle(dve)
                st.by(V.memset(scan[0][:], 0.0))
                st.settle(dve)
                st.by(V.tensor_copy(scan[0][:, :, 1:], groups[:, 0:2, :]))
                st.by(V.tensor_copy(groups[:, REST, :], groups[:, BY_DST, :]))
                st.settle(dve)
                now, step = 0, 1
                while step < NT + 1:
                    src, dst = scan[now], scan[1 - now]
                    st.by(V.tensor_copy(dst[:, :, 0:step], src[:, :, 0:step]))
                    st.by(V.tensor_tensor(dst[:, :, step:], src[:, :, step:], src[:, :, 0:NT + 1 - step], ALU.add))
                    st.settle(dve)
                    now, step = 1 - now, 2 * step
                begin = scan[now]
                st.by(V.tensor_copy(first[:, 0:2, :], begin[:, :, 0:NT]))
                st.by(V.tensor_scalar(first_f[:], begin[:, BY_DST, :], begin[:, BY_DST, ND:ND + 1], None,
                                      ALU.subtract))
                st.settle(dve)
                st.by(V.tensor_copy(first[:, REST, :], first_f[:, 0:NT]))
                st.by(V.tensor_scalar(tot_i[:, 0:2, 0:1], begin[:, :, NT:NT + 1], float(RING - 1), None, ALU.add))
                st.by(V.tensor_scalar(tot_i[:, REST, 0:1], first_f[:, NT:NT + 1], float(RING - 1), None, ALU.add))
                st.settle(dve)
                st.by(V.tensor_scalar(total[:, :, 0:1], tot_i[:, :, 0:1], -RING, None, ALU.bitwise_and))
                st.settle(dve)
                st.by(V.tensor_tensor(groups[:, :, NT - 1:NT], total[:, :, 0:1], first[:, :, NT - 1:NT], ALU.subtract))
                st.by(V.tensor_scalar(tot_i[:, :, 1:2], total[:, :, 0:1], float(G), float(BLOCK + FILL - 1),
                                      ALU.mult, ALU.add))
                st.settle(dve)
                st.by(V.tensor_scalar(total[:, :, 1:2], tot_i[:, :, 1:2], FILL.bit_length() - 1, None,
                                      ALU.logical_shift_right))
                st.settle(dve)
                dve.sem_inc(s_meta, 1)
                st.by(V.memset(running[:], 0.0))
                st.settle(dve)
                for k in range(2):
                    st.by(V.tensor_tensor(tile_pick[:], bc(place_tile[:], 2, [P, NT, NT]),
                                          bc(iota_f[:, 0:NT], 1, [P, NT, NT]), ALU.is_equal))
                    st.settle(dve)
                    st.by(V.tensor_tensor(tile_pick[:], tile_pick[:], bc(begin[:, k, 0:NT], 1, [P, NT, NT]), ALU.mult))
                    st.settle(dve)
                    st.by(V.tensor_reduce(running[:, k, 0, 0:NT], tile_pick[:], AX_X, ALU.add))
                    st.settle(dve)
                    st.by(V.tensor_scalar(count_f[:, k, :], place_part[:], float(COLS), None, ALU.mult))
                    st.settle(dve)
                    st.by(V.scalar_tensor_tensor(running[:, k, 0, 0:NT], running[:, k, 0, 0:NT], float(G),
                                                 count_f[:, k, :], ALU.mult, ALU.add))
                    st.by(V.tensor_copy(running[:, k, 1, 0:NT], place_f[:]))
                    st.by(V.memset(running[0:1, k, 0, NT:HI], float(P * COLS)))
                    st.settle(dve)
                dve.sem_inc(s_meta, 1)

                for k in range(2):
                    dve.sem_inc(s_mask[k], 1)
                    dve.sem_inc(s_taken[k], 1)
                with dve.Fori(0, J_TURNS) as i:
                    st.loop(i, 2 * 3)
                    for b in range(2):
                        for k in range(2):
                            dve.wait_ge(s_run[k], i * (2 * QUAD) + QUAD * (b + 1))
                            cols = bass.ds(i * BODY + b * QUAD, QUAD)
                            V.tensor_tensor(q_lo[b][k][:], bc(lo[:, k, cols], 2, [P, QUAD, P]),
                                            bc(iota_b[:], 1, [P, QUAD, P]), ALU.is_equal)
                            V.tensor_tensor(q_hi[b][k][:], bc(hi[:, k, cols], 2, [P, QUAD, HI]),
                                            bc(iota_b[:, 0:HI], 1, [P, QUAD, HI]), ALU.is_equal).then_inc(s_quad[k], 1)

                    def masks(b):
                        for k in range(2):
                            dve.wait_ge(s_same[k], i * 2 + (b + 1))
                            dve.wait_ge(s_run[k], i * (2 * QUAD) + QUAD * (b + 2))
                            V.tensor_tensor(same[k][:], ps_same[k], bc(earlier_f[:], 1, [P, QUAD, P]),
                                            ALU.mult).then_inc(s_mask[k], 1)

                    def finish(b):
                        for k in range(2):
                            dve.wait_ge(s_found[k], i * 2 + (b + 1))
                            V.tensor_tensor(picked[:, k], ps_found[k].rearrange("p c (w h) -> p c w h", w=2),
                                            bc(q_hi[b][k][:], 2, [P, QUAD, 2, HI]), ALU.mult).then_inc(s_taken[k], 1)
                        for k in range(2):
                            dve.wait_ge(s_taken[k], i * 2 + (b + 2))
                        st.by(V.tensor_reduce(found[:], picked[:], AX_X, ALU.add))
                        st.settle(dve)
                        dve.wait_ge(s_record_free, i * 2 + (b + 1))
                        st.by(V.tensor_copy(slot_no[b][:], found[:, :, :, 0]))
                        for k in range(2):
                            V.tensor_copy(record[b][:, k, :, 0], found[:, 1 - k, :, 1])
                        st.by(V.tensor_copy(record[b][:, :, :, 1],
                                            bc(edge_no[:, bass.ds(i * BODY + b * QUAD, QUAD)], 1, [P, 2, QUAD])))
                        st.settle(dve)
                        dve.sem_inc(s_record, 1)

                    masks(0)
                    masks(1)
                    finish(0)
                    finish(1)
                st.end(J_TURNS)

        if stop_after == "binning":
            return

        PHASES = [
            ("mean", "x0", BY_DST, 0), ("rel_edges_in", "edges", BY_DST, 1), ("rel_edges_out", "edges", BY_SRC, 2),
            ("rel_nodes_in", "x1", REST, None), ("rel_nodes_out", "x1", BY_SRC, None),
            ("att1", "att1", BY_DST, None), ("att2", "att2", BY_DST, None),
            ("pool1", "x3", REST, None), ("pool2", "pool1", REST, None), ("pool3", "top", REST, None),
            ("pool4", "pool3", REST, None)]
        W_ATT = D + 2 * HEADS
        W_HEAD = CH + 1
        tables = {n: dram(f"table_{n}", (NP + 1, W_ATT if n.startswith("att") else D))
                  for n in ("x0", "x1", "att1", "att2", "x3", "pool1", "top", "pool3")}
        adjacency = dram("adjacency", (PIECES, P, NT * WP), BF16)
        adjacency_left = dram("adjacency_left", (PIECES, P, NT * WP), BF16)

        X = sb("X", [P, NT, D])
        Y = sb("Y", [P, NT, D])
        H = sb("H", [P, NT, W_ATT])
        to_logit = sb("to_logit", [P, NT, HEADS])
        node_i = sb("node_i", [P, NT], I32)
        col = {n: sb(f"col_{n}", [P, NT]) for n in
               ("has_in", "w_mean", "w_self", "w_count", "w_deg", "real", "score", "chosen", "t0", "t1")}
        ring = sb("ring", [P, RING, G, W_ATT])
        idx = [sb(f"idx{b}", [P, BLOCK // 2, 2], I32) for b in range(2)]
        empty_row = sb("empty_row", [1, W_ATT])
        MATS = {n: sb(f"w_{n}", [P, D * w]) for n, w in (
            ("mean_self", 1), ("mean_neigh", 1), ("fwd_node", 1), ("fwd_edge", 1), ("back_node", 1),
            ("back_edge", 1), ("att1", 2), ("att2", 1), ("s1", 1), ("n1", 1), ("s2", 1), ("n2", 1),
            ("us1", 1), ("un1", 1), ("us2", 1), ("un2", 1))}
        ROWS = {n: sb(f"r_{n}", [P, D]) for n in (
            "b_mean", "b_fwd", "b_back", "gamma", "beta", "b_att1", "b_att2", "b_res", "b_s1", "b_s2",
            "b_us1", "b_us2", "w_score")}
        att_rows = [sb(f"att_rows{i}", [P, 2, D]) for i in range(2)]
        b_score = sb("b_score", [P, 1])
        eps = sb("eps", [P, 1])

        iota_w = sb("iota_w", [P, WP], I16)
        zeros_w = sb("zeros_w", [P, BANK], BF16)
        src_idx = sb("src_idx", [P, RING, G, 2], I32)
        in_piece = sb("in_piece", [P, G])
        counts = sb("counts", [P, WP], BF16)
        counts_left = sb("counts_left", [P, WP], BF16)
        a_buf = sb("a_buf", [P, 2, SEVEN, WP], BF16)
        parts = sb("parts", [P, 3, NT, D], BF16)
        left = sb("left", [P, SEVEN, D])
        piece_T = sb("piece_T", [P, WP])

        ins = sb("ins", [P, 2, D])
        lhs = sb("lhs", [P, 2, P])
        y = sb("y", [P, D])
        z = sb("z", [P, D])
        stats = sb("stats", [P, 6])
        mean_var = sb("mean_var", [P, 2])
        std = sb("std", [P, 1])
        rstd = sb("rstd", [P, 1])
        logits = sb("logits", [P, G + 1, HEADS])
        raw = sb("raw", [P, G, HEADS])
        peak = sb("peak", [P, HEADS])
        shifted = sb("shifted", [P, G + 1, HEADS])
        probs = sb("probs", [P, G + 1, HEADS])
        weighted = sb("weighted", [P, G + 1, HEADS * W_HEAD])
        att_acc = sb("att_acc", [P, HEADS * W_HEAD])
        tile_logit = sb("tile_logit", [P, HEADS])
        r_sum = sb("r_sum", [P, HEADS])
        both = sb("both", [P, 2, D])
        thr = sb("thr", [P, 1], I32)
        cand = sb("cand", [P, 1], I32)
        bit = sb("bit", [P, 1], I32)
        keep = sb("keep", [P, 1], I32)
        cand_f = sb("cand_f", [P, 1])
        hits = sb("hits", [P, 1])
        need = sb("need", [P, 1])

        s_load = sem("s_load")
        s_ready = sem("s_ready")
        s_dummy = sem("s_dummy")
        s_x = sem("s_x")
        s_idx = [sem(f"s_idx{b}") for b in range(2)]
        s_ring = [sem(f"s_ring{j}") for j in range(RING)]
        s_landed = sem("s_landed")
        s_free = sem("s_free")
        s_sum = sem("s_sum")
        s_src_idx = sem("s_src_idx")
        s_src_free = sem("s_src_free")
        s_hot = sem("s_hot")
        s_hot_free = sem("s_hot_free")
        s_built = sem("s_built")
        s_counts = sem("s_counts")
        s_counts_out = sem("s_counts_out")
        s_left = sem("s_left")
        s_left_out = sem("s_left_out")
        s_bank_free = sem("s_bank_free")
        s_split = sem("s_split")
        s_block = sem("s_block")
        s_block_done = sem("s_block_done")
        s_left_in = sem("s_left_in")
        s_left_done = sem("s_left_done")
        s_piece = sem("s_piece")
        s_piece_T = sem("s_piece_T")
        s_att = sem("s_att")
        s_shift = sem("s_shift")
        s_probs = sem("s_probs")
        s_in = sem("s_in")
        s_tr = sem("s_tr")
        s_lhs = sem("s_lhs")
        s_prod = sem("s_prod")
        s_var = sem("s_var")
        s_std = sem("s_std")
        s_tile = sem("s_tile")
        s_stored = sem("s_stored")
        s_count = sem("s_count")
        s_counted = sem("s_counted")
        s_logit = sem("s_logit")
        s_expd = sem("s_expd")
        s_last = sem("s_last")
        s_out = sem("s_out")
        s_held_pe = sem("s_held_pe")
        s_held_act = sem("s_held_act")

        ps_tr = bank[0][:, 0:2 * P].rearrange("p (j f) -> p j f", j=2)
        ps_prod = bank[1]
        ps_hits = bank[2][:, 0:1]
        ps_sum = bank[3][:, 0:D]
        HALVES = [(0, BANK), (BANK, WP)]
        ps_piece = [[bank[4 + 2 * b + h][:, 0:hi - lo] for h, (lo, hi) in enumerate(HALVES)] for b in range(2)]
        one_hot = a_buf[:].rearrange("p b s w -> p (b s) w")[:, 0:2 * G, :]

        PRODUCTS = {
            "mean": [("mean_self", "mean_neigh")], "rel_nodes_in": [("fwd_node",)], "rel_edges_in": [("fwd_edge",)],
            "rel_edges_out": [("back_edge",)], "rel_nodes_out": [("back_node",), ("att1",)],
            "att1": [("att2",)], "att2": [], "pool1": [("s1", "n1")], "pool2": [("s2", "n2")],
            "pool3": [("us1", "un1")], "pool4": [("us2", "un2")]}
        SCORE_BITS, NODE_BITS = 30, 13
        SEARCH = SCORE_BITS + 1 + NODE_BITS
        N_LOADS = 17 + 13 + 1 + 4
        ACT_STEPS = {"mean": "csw", "rel_nodes_in": "c", "rel_edges_in": "c", "rel_edges_out": "c",
                     "rel_nodes_out": "csscw", "att1": "cw", "att2": "sw", "pool1": "cw", "pool2": "c",
                     "pool3": "cw", "pool4": "cs"}
        STORES = {"mean": ("x1", X, D), "rel_nodes_out": ("att1", H, W_ATT), "att1": ("att2", H, W_ATT),
                  "att2": ("x3", X, D), "pool1": ("pool1", H, D), "pool3": ("pool3", Y, D)}
        SPLIT = {"rel_nodes_in": X, "pool1": X, "pool2": H, "pool3": H, "pool4": Y}
        tile_mark, marks = {}, 0
        for name, _, _, _ in PHASES:
            tile_mark[name] = marks
            if name in STORES:
                marks += NT
            if name == "pool2":
                marks += 1
                tile_mark["top"] = marks
        STEPS = {"mean": 9, "rel_nodes_in": 2, "rel_edges_in": 2, "rel_nodes_out": 27, "rel_edges_out": 2,
                 "att1": 14, "att2": 12, "pool1": 5, "pool2": 7, "pool3": 5, "pool4": 9}
        if stop_after:
            PHASES = PHASES[:[p[0] for p in PHASES].index(stop_after) + 1]

        first_stores = 16 + 16 * (len(tables) + 1)
        stored_by, stores, stored_before = {"x0": first_stores, "edges": first_stores}, first_stores, []
        for name, _, _, _ in PHASES:
            stored_before.append(stores)
            if name in STORES:
                stores += 16 * NT
                stored_by[STORES[name][0]] = stores
            if name == "pool2":
                stores += 16
                stored_by["top"] = stores

        def turns_of(p):
            if PHASES[p][2] != REST:
                return [(NT, 0, None, [(0, False)])]
            return [(SEVEN, ND + SEVEN * i, i if i < PIECES else None,
                     [(ND + SEVEN * i, False)] + ([(SEVEN * (i - 1), True)] if i else []))
                    for i in range(PIECES + 1)]

        def rest_before(p):
            return sum(k == REST for _, _, k, _ in PHASES[:p])

        def sizes(eng):
            return [eng.value_load(total[0:1, k, 0:1], min_val=2 * RING, max_val=(COLS - FILL) // G) for k in range(3)]

        def groups_before(eng, n, p, only=None):
            ks = [k for name, _, k, _ in PHASES[:p] if only is None or name.startswith("att") == only]
            return eng.snap(n[0] * ks.count(BY_DST) + n[1] * ks.count(BY_SRC) + n[2] * ks.count(REST))

        def groups_of(eng, k, t):
            return (eng.value_load(groups[0:1, k, bass.ds(t, 1)], min_val=1, max_val=COLS),
                    eng.value_load(first[0:1, k, bass.ds(t, 1)], min_val=0, max_val=COLS))

        blk = ctx.enter_context(nc.Block())

        @blk.sync
        def _(sp):
            loads = [
                (MATS["mean_self"], a["W0T"][0:D, :]), (MATS["mean_neigh"], a["W0T"][D:2 * D, :]),
                (MATS["fwd_node"], a["WfT"][0:D, :]), (MATS["fwd_edge"], a["WfT"][D:2 * D, :]),
                (MATS["back_node"], a["WbT"][0:D, :]), (MATS["back_edge"], a["WbT"][D:2 * D, :]),
                (MATS["att2"], a["L2_gnn_W2"]),
                (MATS["s1"], a["L3_gnn_ws1"]), (MATS["n1"], a["L3_gnn_wn1"]), (MATS["s2"], a["L3_gnn_ws2"]),
                (MATS["n2"], a["L3_gnn_wn2"]), (MATS["us1"], a["L3_gnn_wu1"]), (MATS["un1"], a["L3_gnn_wnu1"]),
                (MATS["us2"], a["L3_gnn_wu2"]), (MATS["un2"], a["L3_gnn_wnu2"])]
            for dst, src in loads:
                sp.dma_start(dst[:], src).then_inc(s_load, 16)
            sp.dma_start(MATS["att1"][:, 0:D], a["L2_gnn_W1"]).then_inc(s_load, 16)
            sp.dma_start(MATS["att1"][:, D:2 * D], a["L2_gnn_Wr"]).then_inc(s_load, 16)
            rows = [("b_mean", "L0_gnn_b"), ("b_fwd", "L1_gnn_b_fwd"), ("b_back", "L1_gnn_b_back"),
                    ("gamma", "L1_gnn_gamma"), ("beta", "L1_gnn_beta"), ("b_att1", "L2_gnn_b1"),
                    ("b_att2", "L2_gnn_b2"), ("b_res", "L2_gnn_br"), ("b_s1", "L3_gnn_b1"), ("b_s2", "L3_gnn_b2"),
                    ("b_us1", "L3_gnn_bu1"), ("b_us2", "L3_gnn_bu2")]
            for n, src in rows:
                sp.dma_start(ROWS[n][:], a[src].partition_broadcast(P)).then_inc(s_load, 16)
            sp.dma_start(ROWS["w_score"][:], a["L3_gnn_w_score"].rearrange("d o -> (d o)").partition_broadcast(P)
                         ).then_inc(s_load, 16)
            sp.dma_start(b_score[:], a["L3_gnn_b_score"].partition_broadcast(P)).then_inc(s_load, 16)
            for i in range(2):
                for j, end in enumerate(("src", "dst")):
                    sp.dma_start(att_rows[i][:, j, :],
                                 a[f"L2_gnn_a{i + 1}_{end}"].rearrange("h c -> (h c)").partition_broadcast(P)
                                 ).then_inc(s_load, 16)
            sp.wait_ge(s_dummy, 2)
            for t in list(tables.values()) + [edge_rows]:
                rows_of, w = t.shape
                sp.dma_start(t[rows_of - 1:rows_of, :], empty_row[:, 0:w]).then_inc(s_stored, 16)
            sp.wait_ge(s_x, 16 * NT)
            sp.dma_start(tables["x0"][0:NP, :].rearrange("(t p) w -> p t w", p=P), X[:]).then_inc(s_stored, 16)

            n = sizes(sp)
            skipped = sp.value_load(first[0:1, BY_DST, ND:ND + 1], min_val=ND, max_val=COLS // G)
            for p, (name, _, k, _) in enumerate(PHASES):
                base = groups_before(sp, n, p)
                table = slots[BY_SRC if k == BY_SRC else BY_DST][0:P * COLS, :].rearrange("(p c) w -> p c w", p=P)

                def load(turn, b):
                    at = turn * BLOCK + b * (BLOCK // 2)
                    if k == REST:
                        at = nc.s_assert_within(skipped * G + at, 0, COLS - BLOCK,
                                                skip_runtime_bounds_check_because="all groups fit the table")
                    sp.dma_start(idx[b][:], table[:, bass.ds(at, BLOCK // 2), :]).then_inc(s_idx[b], 16)

                def report(turn, b):
                    for j in range(b * RING // 2, (b + 1) * RING // 2):
                        sp.wait_ge(s_ring[j], (base + turn * RING) * (16 * G // RING) + 16 * G)
                        sp.sem_inc(s_landed, 1)

                load(0, 0)
                load(0, 1)
                turns = sp.snap(n[k] // RING)
                with sp.Fori(0, turns - 1) as i:
                    for b in range(2):
                        report(i, b)
                        load(i + 1, b)
                for b in range(2):
                    report(turns - 1, b)
                if name == "pool2":
                    sp.wait_ge(s_tile, tile_mark["top"])
                    sp.dma_start(tables["top"][0:NP, :].rearrange("(t p) w -> p t w", p=P), H[:, :, 0:D]
                                 ).then_inc(s_stored, 16)

        @blk.gpsimd
        def _(pool):
            nc.gpsimd.memset(empty_row[:], 0.0).then_inc(s_dummy, 1)
            pool.wait_ge(s_dummy, 1)
            nc.gpsimd.memset(empty_row[:, HEADS * W_HEAD:], FAR).then_inc(s_dummy, 1)
            nc.gpsimd.iota(iota_w[:], [[1, WP]], base=0, channel_multiplier=0).then_inc(s_dummy, 1)
            nc.gpsimd.memset(zeros_w[:], 0.0).then_inc(s_dummy, 1)
            pool.wait_ge(s_ready, 1)
            for t in range(NT):
                pool.indirect_dma_start(
                    out=X[:, t, :], out_offset=None, in_=a["x"],
                    in_offset=bass.IndirectOffsetOnAxis(ap=node_i[:, t:t + 1], axis=0),
                    bounds_check=N - 1, oob_is_err=False).then_inc(s_x, 16)
            n = sizes(pool)
            pool.wait_ge(s_edges, 16 * (E // EDGE_COPY))
            for p, (name, source, k, _) in enumerate(PHASES):
                base = groups_before(pool, n, p)
                turns_before = pool.snap(base // RING)
                pool.wait_ge(s_stored, stored_by[source])
                with pool.Fori(0, n[k] // RING) as i:
                    for j in range(RING):
                        b, c = divmod(j * G, BLOCK // 2)
                        if c == 0:
                            hold(pool, s_idx[b], (turns_before + i) * 16 + 16, s_held_pool)
                        hold(pool, s_free, (base + i * RING) + (j + 1), s_held_pool)
                        for g in range(G):
                            rows, which = (edge_rows, 1) if source == "edges" else (tables[source], 0)
                            pool.indirect_dma_start(
                                out=ring[:, j, g, 0:rows.shape[1]], out_offset=None, in_=rows,
                                in_offset=bass.IndirectOffsetOnAxis(ap=idx[b][:, c + g, which:which + 1], axis=0),
                                ).then_inc(s_ring[j], 16)
            if not stop_after:
                pool.wait_ge(s_last, 1)
                for t in range(NT):
                    pool.indirect_dma_start(
                        out=out, out_offset=bass.IndirectOffsetOnAxis(ap=node_i[:, t:t + 1], axis=0),
                        in_=X[:, t, :], in_offset=None, bounds_check=N - 1, oob_is_err=False).then_inc(s_out, 16)
                pool.wait_ge(s_out, 16 * NT)

        @blk.tensor
        def _(pe):
            pe.wait_ge(s_load, 16 * N_LOADS)
            pe.wait_ge(s_dummy, 4)
            n = sizes(pe)
            is_large = pe.value_load(large[0:1, 0:1], min_val=0, max_val=1)
            products, blocks = 0, 0

            def zero(ps, w):
                nc.tensor.matmul(ps, zeros_b[:], zeros_w[:, 0:w], start=True, stop=False, skip_group_check=True)

            def close(ps, signal):
                nc.tensor.matmul(ps[:, 0:1], zeros_b[:], zeros_w[:, 0:1], start=False, stop=True,
                                 skip_group_check=True).then_inc(signal, 1)

            def multiply(dst, u, buf):
                for s in range(SEVEN):
                    for part in range(3):
                        for h, (lo, hi) in enumerate(HALVES):
                            mm = nc.tensor.matmul(
                                dst[h], parts[:, part, bass.ds(u * SEVEN + s, 1), :].rearrange("p a f -> p (a f)"),
                                a_buf[:, buf, s, lo:hi].rearrange("p a w -> p (a w)"),
                                start=False, stop=False, skip_group_check=True)
                return mm

            for p, (name, source, k, piece) in enumerate(PHASES):
                att = name.startswith("att")
                base = groups_before(pe, n, p)
                apart = name.startswith("pool")
                for trips, tile0, mul, stages in turns_of(p):
                    per = len(PRODUCTS[name]) * len(stages)
                    if mul is not None:
                        b = mul & 1
                        if blocks == 0:
                            pe.wait_ge(s_counts, PIECES * NT + 1)
                            pe.wait_ge(s_bank_free, PIECES * NT + 1)
                        elif blocks > SEVEN:
                            pe.wait_ge(s_piece_T, blocks // SEVEN - (mul > 0))
                        for h, (lo, hi) in enumerate(HALVES):
                            zero(ps_piece[b][h], hi - lo)
                    if per or not att:
                        with pe.Fori(0, trips) as t:
                            if not att:
                                mine, start = groups_of(pe, k, t + tile0)
                                arrived = pe.snap(base + start)
                                zero(ps_sum, D)
                                with pe.Fori(0, mine) as g:
                                    hold(pe, s_landed, arrived + g + 1, s_held_pe)
                                    entry = bass.ds((arrived + g) & (RING - 1), 1)
                                    for c in range(G):
                                        mm = nc.tensor.matmul(ps_sum, ident[:],
                                                              ring[:, entry, c, 0:D].rearrange("p a w -> p (a w)"),
                                                              start=False, stop=False, skip_group_check=True)
                                    mm.then_inc(s_free, 1)
                                close(ps_sum, s_sum)
                            if piece is not None:
                                mine, start = groups_of(pe, BY_SRC, t)
                                at = pe.snap(n[BY_SRC] * piece + start)
                                hold(pe, s_counts, t + (piece * NT + 1), s_held_pe)
                                hold(pe, s_bank_free, t + (piece * NT + 1), s_held_pe)
                                for h, (lo, hi) in enumerate(HALVES):
                                    zero(ps_piece[0][h], hi - lo)
                                with pe.Fori(0, mine) as g:
                                    hold(pe, s_hot, (at + g) * (G + 1) + (G + 1), s_held_pe)
                                    b0 = pe.snap(((at + g) & 1) * G)
                                    for c in range(G):
                                        for h, (lo, hi) in enumerate(HALVES):
                                            mm = nc.tensor.matmul(
                                                ps_piece[0][h], ident_b[:],
                                                one_hot[:, bass.ds(b0 + c, 1), lo:hi].rearrange("p a w -> p (a w)"),
                                                start=False, stop=False, skip_group_check=True)
                                    mm.then_inc(s_hot_free, 1)
                                close(ps_piece[0][0], s_built)
                            if mul is not None:
                                hold(pe, s_split, t + (rest_before(p) * SEVEN + 1) if mul == 0
                                     else (rest_before(p) + 1) * SEVEN, s_held_pe)
                                hold(pe, s_block, t * 16 + 16 * (blocks + 1), s_held_pe)
                                buf = bass.ds((t + blocks) & 1, 1)
                                multiply(ps_piece[b], t, buf).then_inc(s_block_done, 1)
                                with pe.If(is_large > 0):
                                    hold(pe, s_left_in, t * 16 + 16 * (blocks + 1), s_held_pe)
                                    multiply(ps_piece[b], t, buf).then_inc(s_left_done, 1)
                                pe.end_ifs()
                            done = 0
                            for _, from_piece in stages:
                                for mats in PRODUCTS[name]:
                                    done += 1
                                    pe.wait_ge(s_in, t * per + (products + done))
                                    if from_piece and name == "rel_nodes_in":
                                        pe.sem_inc(s_tr, 1)
                                    else:
                                        for j in range(1 if from_piece else len(mats)):
                                            mm = nc.tensor.transpose(ps_tr[:, j, :], ins[:, j, :], ident[:])
                                        mm.then_inc(s_tr, 1)
                                    pe.wait_ge(s_lhs, t * per + (products + done))
                                    for j, m in enumerate(mats):
                                        w = MATS[m].shape[1]
                                        to = j * D if apart else 0
                                        mm = nc.tensor.matmul(ps_prod[:, to:to + w], lhs[:, j, :], MATS[m][:],
                                                              start=(apart or j == 0),
                                                              stop=(apart or j == len(mats) - 1))
                                    mm.then_inc(s_prod, 1)
                    products += per * trips
                    if mul is not None:
                        blocks += SEVEN
                        close(ps_piece[b][0], s_piece)
                if name == "pool2":
                    with pe.Fori(0, SEARCH) as i:
                        pe.wait_ge(s_count, i + 1)
                        nc.tensor.matmul(ps_hits, ones[:], hits[:], start=True, stop=True).then_inc(s_counted, 1)

        @blk.scalar
        def _(act):
            copies, roots, writes, blocks = 0, 0, 0, 0
            n = sizes(act)
            is_large = act.value_load(large[0:1, 0:1], min_val=0, max_val=1)
            act.sem_inc(s_counts, 1)
            rest_phases = sum(k == REST for _, _, k, _ in PHASES)

            def load_block(matrix, mul, u, buf, signal):
                act.dma_start(a_buf[:, buf, :, :].rearrange("p a s w -> p (a s w)"),
                              matrix[mul % PIECES, :, bass.ds(u * (SEVEN * WP), SEVEN * WP)]).then_inc(signal, 16)

            for p, (name, _, k, piece) in enumerate(PHASES):
                steps = ACT_STEPS[name]
                if k == REST and blocks == 0:
                    act.wait_ge(s_counts_out, 16 * PIECES * NT + 16)
                    with act.If(is_large > 0):
                        act.wait_ge(s_left_out, 16 * PIECES * NT + 16)
                        act.sem_inc(s_held_act, 1)
                    act.end_ifs()
                    act.wait_ge(s_built, PIECES * NT)
                    load_block(adjacency, 0, 0, bass.ds(0, 1), s_block)
                    act.wait_ge(s_block, 16)
                    load_block(adjacency, 0, 1, bass.ds(1, 1), s_block)
                for trips, tile0, mul, stages in turns_of(p):
                    nc_, ns_, nw_ = (steps.count(w) * len(stages) for w in "csw")
                    if stages[-1][1]:
                        act.wait_ge(s_piece_T, blocks // SEVEN)
                    for lo_t, hi_t in ([(0, SEVEN - 2), (SEVEN - 2, SEVEN)] if mul is not None else [(0, trips)]):
                        with act.Fori(lo_t, hi_t) as t:
                            if piece is not None:
                                mine, start = groups_of(act, BY_SRC, t)
                                at = act.snap(n[BY_SRC] * piece + start)
                                table = slots[BY_SRC][0:P * COLS, :].rearrange("(p c) w -> p c w", p=P)
                                with act.Fori(0, mine) as g:
                                    hold(act, s_src_free, at + g + 1, s_held_act)
                                    act.wait_ge(s_src_idx, (at + g) * 16 + 16)
                                    slot = nc.s_assert_within((start + g) * G, 0, COLS - G,
                                                              skip_runtime_bounds_check_because="all groups fit the table")
                                    act.dma_start(
                                        src_idx[:, bass.ds((at + g) & (RING - 1), 1), :, :].rearrange(
                                            "p a g w -> p (a g) w"),
                                        table[:, bass.ds(slot, G), :]).then_inc(s_src_idx, 16)
                                hold(act, s_built, t + (piece * NT + 1), s_held_act)
                                hold(act, s_counts_out, t * 16 + (piece * NT * 16 + 16), s_held_act)
                                nc.scalar.copy(counts[:, 0:BANK], ps_piece[0][0])
                                nc.scalar.copy(counts[:, BANK:WP], ps_piece[0][1]).then_inc(s_counts, 1)
                                act.wait_ge(s_counts, t + (piece * NT + 2))
                                act.dma_start(adjacency[piece, :, bass.ds(t * WP, WP)], counts[:]
                                              ).then_inc(s_counts_out, 16)
                            if mul is not None:
                                buf = bass.ds((t + blocks) & 1, 1)
                                hold(act, s_block_done, t + (blocks + 1), s_held_act)
                                with act.If(is_large > 0):
                                    load_block(adjacency_left, mul, t, buf, s_left_in)
                                    hold(act, s_left_done, t + (blocks + 1), s_held_act)
                                act.end_ifs()
                                if lo_t == 0 or mul < PIECES - 1 or rest_before(p) < rest_phases - 1:
                                    act.wait_ge(s_block, t * 16 + 16 * (blocks + 2))
                                    if lo_t == 0:
                                        load_block(adjacency, mul, t + 2, buf, s_block)
                                    else:
                                        load_block(adjacency, mul + 1, t - (SEVEN - 2), buf, s_block)
                            if name.startswith("att"):
                                base = groups_before(act, n, p, True)
                                mine, start = groups_of(act, k, t)
                                at = act.snap(base + start)
                                with act.Fori(0, mine) as g:
                                    act.wait_ge(s_shift, at + g + 1)
                                    nc.scalar.activation(probs[:], shifted[:], ACT.Exp).then_inc(s_probs, 1)
                            ci, si = 0, 0
                            for stage, (stage0, from_piece) in enumerate(stages):
                                j = 0
                                for what in steps:
                                    if what == "c":
                                        m = len(PRODUCTS[name][j])
                                        ci, j = ci + 1, j + 1
                                        act.wait_ge(s_tr, t * nc_ + (copies + ci))
                                        if from_piece and m == 2:
                                            nc.scalar.copy(lhs[:, 0, :], ps_tr[:, 0, :])
                                        if from_piece:
                                            nc.scalar.copy(lhs[:, m - 1, :], piece_T[:, bass.ds(t * P, P)]
                                                           ).then_inc(s_lhs, 1)
                                        else:
                                            nc.scalar.copy(lhs[:, 0:m, :], ps_tr[:, 0:m, :]).then_inc(s_lhs, 1)
                                    elif what == "s":
                                        si += 1
                                        act.wait_ge(s_var, t * ns_ + (roots + si))
                                        nc.scalar.activation(std[:], mean_var[:, 1:2], ACT.Sqrt, bias=eps[:]
                                                             ).then_inc(s_std, 1)
                                    else:
                                        table, state, w = STORES[name]
                                        act.wait_ge(s_tile, t * nw_ + (writes + stage + 1))
                                        act.dma_start(tables[table][bass.ds(t * P + stage0 * P, P), :],
                                                      state[:, bass.ds(t + stage0, 1), 0:w].rearrange("p a w -> p (a w)")
                                                      ).then_inc(s_stored, 16)
                            if piece is not None:
                                with act.If(is_large > 0):
                                    hold(act, s_left, t + (piece * NT + 1), s_held_act)
                                    act.dma_start(adjacency_left[piece, :, bass.ds(t * WP, WP)], counts_left[:]
                                                  ).then_inc(s_left_out, 16)
                                act.end_ifs()
                    copies, roots, writes = copies + trips * nc_, roots + trips * ns_, writes + trips * nw_
                    if mul is not None:
                        blocks += SEVEN
                        act.wait_ge(s_piece, blocks // SEVEN)
                        nc.scalar.copy(piece_T[:, 0:BANK], ps_piece[mul & 1][0])
                        nc.scalar.copy(piece_T[:, BANK:WP], ps_piece[mul & 1][1]).then_inc(s_piece_T, 1)
                if name == "pool2":
                    writes += 1
                    act.wait_ge(s_logit, 1)
                    nc.scalar.activation(col["t0"][:], col["score"][:], ACT.Exp, scale=-1.0).then_inc(s_expd, 1)

        @blk.vector
        def _(dve):
            V = nc.vector
            used = {"in": 0, "var": 0}

            st.by(V.tensor_copy(node_i[:], by_place[:, :, 2]))
            st.by(V.memset(X[:], 0.0))
            st.by(V.memset(eps[:], LN_EPS))
            st.by(V.memset(H[:], 1.0))
            st.settle(dve)
            dve.sem_inc(s_ready, 1)
            dve.sem_inc(s_free, RING)
            dve.sem_inc(s_src_free, RING)
            dve.sem_inc(s_src_idx, 16)
            dve.sem_inc(s_hot_free, 2)
            dve.sem_inc(s_counts_out, 16)
            dve.sem_inc(s_left_out, 16)
            dve.sem_inc(s_bank_free, 1)
            din, dout, node = (by_place[:, :, j] for j in range(3))
            st.by(V.tensor_scalar(col["has_in"][:], din, 0.0, None, ALU.is_gt))
            st.by(V.tensor_scalar(col["w_self"][:], din, 0.0, None, ALU.is_equal))
            st.by(V.tensor_scalar(col["t0"][:], din, 1.0, None, ALU.max))
            st.by(V.tensor_scalar(col["real"][:], node, float(N), None, ALU.is_lt))
            st.by(V.tensor_tensor(col["t1"][:], din, dout, ALU.add))
            st.settle(dve)
            st.by(V.reciprocal(col["w_deg"][:], col["t0"][:]))
            st.by(V.tensor_tensor(col["t1"][:], col["t1"][:], col["real"][:], ALU.subtract))
            st.settle(dve)
            st.by(V.tensor_tensor(col["w_mean"][:], col["w_deg"][:], col["has_in"][:], ALU.mult))
            st.by(V.tensor_scalar(col["t1"][:], col["t1"][:], 1.0, None, ALU.add))
            st.settle(dve)
            st.by(V.reciprocal(col["w_count"][:], col["t1"][:]))
            st.settle(dve)
            dve.wait_ge(s_load, 16 * N_LOADS)
            dve.wait_ge(s_dummy, 4)
            dve.wait_ge(s_x, 16 * NT)

            n = sizes(dve)
            is_large = dve.value_load(large[0:1, 0:1], min_val=0, max_val=1)
            sums = 0
            for p, (name, source, k, piece) in enumerate(PHASES):
                att = name.startswith("att")
                dve.wait_ge(s_stored, stored_before[p])
                base = groups_before(dve, n, p)
                mine_before = groups_before(dve, n, p, att)
                loop_steps = STEPS[name]
                for trips, tile0, mul, stages in turns_of(p):
                    per_in = len(PRODUCTS[name]) * len(stages)
                    per_var = ACT_STEPS[name].count("s") * len(stages)
                    seen = {"in": 0, "var": 0}
                    with dve.Fori(0, trips) as t:
                        st.loop(t, loop_steps * len(stages) + (5 if mul == 0 else 0))

                        def product():
                            seen["in"] += 1
                            st.settle(dve)
                            dve.sem_inc(s_in, 1)
                            hold(dve, s_prod, t * per_in + (used["in"] + seen["in"]), s_held_dve)

                        def norm(dst, src):
                            seen["var"] += 1
                            st.by(V.bn_stats(stats[:], src))
                            st.settle(dve, s_held_dve)
                            st.by(V.bn_aggr(mean_var[:], stats[:]))
                            st.settle(dve)
                            dve.sem_inc(s_var, 1)
                            dve.wait_ge(s_std, t * per_var + (used["var"] + seen["var"]))
                            st.by(V.reciprocal(rstd[:], std[:]))
                            st.settle(dve)
                            st.by(V.tensor_scalar(dst, src, mean_var[:, 0:1], rstd[:], ALU.subtract, ALU.mult))
                            st.settle(dve, s_held_dve)

                        def heads(ap):
                            return ap.rearrange("p (h c) -> p h c", h=HEADS)

                        if mul == 0:
                            block = bass.ds(t * SEVEN, SEVEN)
                            st.by(V.tensor_copy(parts[:, 0, block, :], SPLIT[name][:, block, 0:D]))
                            st.settle(dve)
                            st.by(V.tensor_tensor(left[:], SPLIT[name][:, block, 0:D], parts[:, 0, block, :],
                                                  ALU.subtract))
                            st.settle(dve)
                            st.by(V.tensor_copy(parts[:, 1, block, :], left[:]))
                            st.settle(dve)
                            st.by(V.tensor_tensor(left[:], left[:], parts[:, 1, block, :], ALU.subtract))
                            st.settle(dve)
                            st.by(V.tensor_copy(parts[:, 2, block, :], left[:]))
                            st.settle(dve)
                            dve.sem_inc(s_split, 1)

                        if piece is not None:
                            mine, start = groups_of(dve, BY_SRC, t)
                            at_src = dve.snap(n[BY_SRC] * piece + start)
                            with dve.Fori(0, mine) as g:
                                hot = Count(s_hot)
                                hot.loop(at_src + g, G + 1)
                                hold(dve, s_src_idx, (at_src + g) * 16 + 32, s_held_dve)
                                entry = bass.ds((at_src + g) & (RING - 1), 1)
                                b0 = dve.snap(((at_src + g) & 1) * G)
                                hot.by(V.tensor_scalar(in_piece[:], src_idx[:, entry, :, 0].rearrange("p a g -> p (a g)"),
                                                       float(-piece * WP), None, ALU.add))
                                hot.settle(dve)
                                dve.sem_inc(s_src_free, 1)
                                hold(dve, s_hot_free, at_src + g + 1, s_held_dve)
                                for c in range(G):
                                    hot.by(V.tensor_scalar(one_hot[:, bass.ds(b0 + c, 1), :].rearrange("p a w -> p (a w)"),
                                                           iota_w[:], in_piece[:, c:c + 1], None, ALU.is_equal))
                                hot.settle(dve)

                        for stage, (stage0, from_piece) in enumerate(stages):
                            tt = t + stage0
                            at = bass.ds(tt, 1)

                            def tile(state, w=D):
                                return state[:, at, 0:w].rearrange("p a w -> p (a w)")

                            def one(c):
                                return col[c][:, at]

                            def logits_of(i):
                                feats = H[:, at, 0:HEADS * W_HEAD].rearrange("p a (h c) -> p (a h) c", h=HEADS)[:, :, 0:CH]
                                for j in range(2):
                                    st.by(V.tensor_tensor(both[:, j, :].rearrange("p (h c) -> p h c", h=HEADS), feats,
                                                          att_rows[i][:, j, :].rearrange("p (h c) -> p h c", h=HEADS),
                                                          ALU.mult))
                                st.settle(dve, s_held_dve)
                                st.by(V.tensor_reduce(H[:, at, HEADS * W_HEAD:].rearrange("p a h -> p (a h)"),
                                                      both[:, 0, :].rearrange("p (h c) -> p h c", h=HEADS), AX_X, ALU.add))
                                st.by(V.tensor_reduce(to_logit[:, at, :].rearrange("p a h -> p (a h)"),
                                                      both[:, 1, :].rearrange("p (h c) -> p h c", h=HEADS), AX_X, ALU.add))

                            if att:
                                st.by(V.tensor_copy(tile_logit[:], to_logit[:, at, :].rearrange("p a h -> p (a h)")))
                                st.by(V.tensor_copy(att_acc[:], tile(H, HEADS * W_HEAD)))
                                st.by(V.tensor_copy(peak[:], H[:, at, HEADS * W_HEAD:].rearrange("p a h -> p (a h)")))
                                st.settle(dve)
                                st.by(V.tensor_tensor(peak[:], peak[:], tile_logit[:], ALU.add))
                                st.settle(dve)
                                st.by(V.scalar_tensor_tensor(logits[:, G, :], peak[:], 0.2, peak[:], ALU.mult, ALU.max))
                                st.settle(dve)
                                mine, start = groups_of(dve, k, t)
                                arrived = dve.snap(base + start)
                                steps_at = dve.snap(mine_before + start)
                                with dve.Fori(0, mine) as g:
                                    inner = Count(s_att)
                                    inner.loop(steps_at + g, 7)
                                    hold(dve, s_landed, arrived + g + 1, None)
                                    entry = bass.ds((arrived + g) & (RING - 1), 1)
                                    rows = ring[:, entry, :, :].rearrange("p a g w -> p (a g) w")
                                    inner.by(V.tensor_tensor(raw[:], rows[:, :, HEADS * W_HEAD:],
                                                             bc(tile_logit[:], 1, [P, G, HEADS]), ALU.add))
                                    inner.settle(dve)
                                    inner.by(V.scalar_tensor_tensor(logits[:, 0:G, :], raw[:], 0.2, raw[:], ALU.mult,
                                                                    ALU.max))
                                    inner.settle(dve)
                                    inner.by(V.tensor_reduce(peak[:], logits[:].rearrange("p g h -> p h g"), AX_X, ALU.max))
                                    inner.settle(dve)
                                    V.tensor_tensor(shifted[:], logits[:], bc(peak[:], 1, [P, G + 1, HEADS]),
                                                    ALU.subtract).then_inc(s_shift, 1)
                                    dve.wait_ge(s_probs, steps_at + g + 1)
                                    inner.by(V.tensor_copy(logits[:, G, :], peak[:]))
                                    inner.by(V.tensor_tensor(
                                        weighted[:, 0:G, :].rearrange("p g (h c) -> p g h c", h=HEADS),
                                        rows[:, :, 0:HEADS * W_HEAD].rearrange("p g (h c) -> p g h c", h=HEADS),
                                        bc(probs[:, 0:G, :], 3, [P, G, HEADS, W_HEAD]), ALU.mult))
                                    inner.by(V.tensor_tensor(heads(weighted[:, G, :]), heads(att_acc[:]),
                                                             bc(probs[:, G, :], 2, [P, HEADS, W_HEAD]), ALU.mult))
                                    inner.settle(dve)
                                    dve.sem_inc(s_free, 1)
                                    inner.by(V.tensor_reduce(att_acc[:], weighted[:].rearrange("p g f -> p f g"), AX_X,
                                                             ALU.add))
                                    inner.settle(dve)
                                    assert inner.k == inner.per, inner.k
                            elif not from_piece:
                                hold(dve, s_sum, t + (sums + 1), s_held_dve)

                            if name == "mean":
                                st.by(V.tensor_copy(ins[:, 0, :], tile(X)))
                                st.by(V.tensor_scalar(y[:], tile(X), one("w_self"), None, ALU.mult))
                                st.settle(dve)
                                st.by(V.scalar_tensor_tensor(ins[:, 1, :], ps_sum, one("w_mean"), y[:], ALU.mult, ALU.add))
                                product()
                                st.by(V.tensor_tensor(y[:], ps_prod[:, 0:D], ROWS["b_mean"][:], ALU.add))
                                st.settle(dve)
                                st.by(V.scalar_tensor_tensor(y[:], y[:], 0.0, tile(X), ALU.max, ALU.add))
                                st.settle(dve)
                                norm(tile(X), y[:])
                                dve.sem_inc(s_tile, 1)
                            elif name.startswith("rel_"):
                                if not from_piece:
                                    st.by(V.tensor_copy(ins[:, 0, :], ps_sum))
                                product()
                                if name == "rel_edges_in":
                                    st.by(V.tensor_copy(tile(Y), ps_prod[:, 0:D]))
                                else:
                                    st.by(V.tensor_tensor(tile(Y), tile(Y), ps_prod[:, 0:D], ALU.add))
                                if from_piece:
                                    st.by(V.memset(y[:, 0:1], 0.0))
                                st.settle(dve)
                                if name == "rel_nodes_out":
                                    st.by(V.scalar_tensor_tensor(y[:], ROWS["b_fwd"][:], by_place[:, at, 0], tile(Y),
                                                                 ALU.mult, ALU.add))
                                    st.settle(dve)
                                    st.by(V.scalar_tensor_tensor(y[:], ROWS["b_back"][:], by_place[:, at, 1], y[:],
                                                                 ALU.mult, ALU.add))
                                    st.settle(dve)
                                    st.by(V.tensor_scalar(y[:], y[:], one("w_count"), None, ALU.mult))
                                    st.settle(dve)
                                    st.by(V.scalar_tensor_tensor(y[:], y[:], 0.01, y[:], ALU.mult, ALU.max))
                                    st.settle(dve)
                                    st.by(V.tensor_tensor(y[:], y[:], tile(X), ALU.add))
                                    st.settle(dve)
                                    norm(z[:], y[:])
                                    st.by(V.tensor_tensor(z[:], z[:], ROWS["gamma"][:], ALU.mult))
                                    st.settle(dve)
                                    st.by(V.tensor_tensor(z[:], z[:], ROWS["beta"][:], ALU.add))
                                    st.settle(dve)
                                    st.by(V.tensor_tensor(y[:], z[:], tile(X), ALU.add))
                                    st.settle(dve)
                                    norm(tile(X), y[:])
                                    st.by(V.tensor_copy(ins[:, 0, :], tile(X)))
                                    product()
                                    st.by(V.tensor_copy(heads(tile(H, HEADS * W_HEAD))[:, :, 0:CH], heads(ps_prod[:, 0:D])))
                                    st.by(V.tensor_tensor(y[:], ps_prod[:, D:2 * D], tile(X), ALU.add))
                                    st.settle(dve)
                                    st.by(V.tensor_tensor(y[:], y[:], ROWS["b_res"][:], ALU.add))
                                    st.settle(dve)
                                    st.by(V.tensor_tensor(tile(Y), y[:], ROWS["b_att2"][:], ALU.add))
                                    logits_of(0)
                                    st.settle(dve)
                                    dve.sem_inc(s_tile, 1)
                            elif att:
                                st.by(V.reciprocal(r_sum[:], heads(att_acc[:])[:, :, CH]))
                                st.settle(dve)
                                st.by(V.tensor_tensor(heads(y[:]), heads(att_acc[:])[:, :, 0:CH],
                                                      bc(r_sum[:], 2, [P, HEADS, CH]), ALU.mult))
                                st.settle(dve)
                                if name == "att1":
                                    st.by(V.tensor_tensor(y[:], y[:], ROWS["b_att1"][:], ALU.add))
                                    st.settle(dve)
                                    st.by(V.tensor_scalar(ins[:, 0, :], y[:], 0.0, None, ALU.max))
                                    product()
                                    st.by(V.tensor_copy(heads(tile(H, HEADS * W_HEAD))[:, :, 0:CH], heads(ps_prod[:, 0:D])))
                                    st.settle(dve)
                                    logits_of(1)
                                    st.settle(dve)
                                else:
                                    st.by(V.tensor_tensor(y[:], y[:], tile(Y), ALU.add))
                                    st.settle(dve)
                                    norm(tile(X), y[:])
                                dve.sem_inc(s_tile, 1)
                            else:
                                state = {"pool1": X, "pool2": H, "pool3": H, "pool4": Y}[name]
                                st.by(V.tensor_copy(ins[:, 0, :], tile(state)))
                                if from_piece:
                                    st.by(V.memset(z[:, 0:1], 0.0))
                                else:
                                    st.by(V.tensor_copy(ins[:, 1, :], ps_sum))
                                product()
                                bias = ROWS[{"pool1": "b_s1", "pool2": "b_s2", "pool3": "b_us1", "pool4": "b_us2"}[name]]
                                st.by(V.scalar_tensor_tensor(y[:], ps_prod[:, D:2 * D], one("w_deg"), bias[:],
                                                             ALU.mult, ALU.add))
                                st.settle(dve)
                                st.by(V.tensor_tensor(y[:], y[:], ps_prod[:, 0:D], ALU.add))
                                st.settle(dve)
                                if name in ("pool1", "pool3"):
                                    target = H if name == "pool1" else Y
                                    st.by(V.tensor_scalar(tile(target), y[:], 0.0, None, ALU.max))
                                    st.settle(dve)
                                    dve.sem_inc(s_tile, 1)
                                elif name == "pool2":
                                    st.by(V.tensor_tensor(z[:], y[:], ROWS["w_score"][:], ALU.mult))
                                    st.by(V.tensor_copy(tile(Y), y[:]))
                                    st.settle(dve, s_held_dve)
                                    st.by(V.tensor_reduce(one("score"), z[:], AX_X, ALU.add))
                                    st.settle(dve)
                                else:
                                    st.by(V.tensor_tensor(y[:], y[:], tile(X), ALU.add))
                                    st.settle(dve)
                                    norm(tile(X), y[:])

                        if piece is not None:
                            dve.sem_inc(s_held_dve, 1)
                            with dve.If(is_large > 0):
                                hold(dve, s_counts, t + (piece * NT + 2), s_held_dve)
                                hold(dve, s_left_out, t * 16 + (piece * NT * 16 + 16), s_held_dve)
                                V.tensor_tensor(counts_left[:, 0:BANK], ps_piece[0][0], counts[:, 0:BANK], ALU.subtract)
                                V.tensor_tensor(counts_left[:, BANK:WP], ps_piece[0][1], counts[:, BANK:WP],
                                                ALU.subtract).then_inc(s_left, 1)
                                hold(dve, s_left, t + (piece * NT + 1), s_held_dve)
                            dve.end_ifs()
                            dve.sem_inc(s_bank_free, 1)
                    used["in"] += trips * per_in
                    used["var"] += trips * per_var
                    sums += 0 if att else trips
                    st.end(trips)

                if name == "pool2":
                    score, chosen, t0, t1 = (col[c][:] for c in ("score", "chosen", "t0", "t1"))
                    st.by(V.tensor_scalar(score, score, b_score[:], None, ALU.add))
                    st.settle(dve)
                    dve.sem_inc(s_logit, 1)
                    dve.wait_ge(s_expd, 1)
                    st.by(V.tensor_scalar(t0, t0, 1.0, None, ALU.add))
                    st.settle(dve)
                    st.by(V.reciprocal(t1, t0))
                    st.settle(dve)
                    st.by(V.tensor_tensor(t0, t1, col["real"][:], ALU.mult))
                    st.by(V.tensor_scalar(score, col["real"][:], -1.0, None, ALU.add))
                    st.settle(dve)
                    st.by(V.tensor_tensor(score, score, t0, ALU.add))
                    st.by(V.memset(thr[:], 0))
                    st.by(V.memset(bit[:], 1 << SCORE_BITS))
                    st.settle(dve)

                    def search(trips, offset, count_hits, limit, op):
                        with dve.Fori(0, trips) as i:
                            st.loop(i, 7 if trips == SCORE_BITS else 9)
                            st.by(V.tensor_scalar(bit[:], bit[:], 1, None, ALU.logical_shift_right))
                            st.settle(dve)
                            st.by(V.tensor_tensor(cand[:], thr[:], bit[:], ALU.bitwise_or))
                            st.settle(dve)
                            count_hits()
                            st.by(V.tensor_reduce(hits[:], t0, AX_X, ALU.add))
                            st.settle(dve)
                            dve.sem_inc(s_count, 1)
                            dve.wait_ge(s_counted, i + (offset + 1))
                            st.by(V.tensor_scalar(keep[:], ps_hits, limit, -1.0, op, ALU.mult))
                            st.settle(dve)
                            st.by(V.tensor_tensor(keep[:], keep[:], bit[:], ALU.bitwise_and))
                            st.settle(dve)
                            st.by(V.tensor_tensor(thr[:], thr[:], keep[:], ALU.bitwise_or))
                            st.settle(dve)
                        st.end(trips)

                    def above():
                        st.by(V.tensor_scalar(t0, score, cand[:].bitcast(F32), None, ALU.is_ge))
                        st.settle(dve)

                    def ties_before():
                        st.by(V.tensor_copy(cand_f[:], cand[:]))
                        st.settle(dve)
                        st.by(V.tensor_scalar(t0, node, cand_f[:], None, ALU.is_lt))
                        st.settle(dve)
                        st.by(V.tensor_tensor(t0, t0, t1, ALU.mult))
                        st.settle(dve)

                    search(SCORE_BITS, 0, above, float(TOP), ALU.is_ge)
                    st.by(V.tensor_scalar(chosen, score, thr[:].bitcast(F32), None, ALU.is_gt))
                    st.by(V.tensor_scalar(t1, score, thr[:].bitcast(F32), None, ALU.is_equal))
                    st.settle(dve)
                    st.by(V.tensor_reduce(hits[:], chosen, AX_X, ALU.add))
                    st.by(V.memset(thr[:], 0))
                    st.by(V.memset(bit[:], 1 << NODE_BITS))
                    st.settle(dve)
                    dve.sem_inc(s_count, 1)
                    dve.wait_ge(s_counted, SCORE_BITS + 1)
                    st.by(V.tensor_scalar(need[:], ps_hits, -1.0, float(TOP), ALU.mult, ALU.add))
                    st.settle(dve)
                    search(NODE_BITS, SCORE_BITS + 1, ties_before, need[:], ALU.is_le)
                    st.by(V.tensor_copy(cand_f[:], thr[:]))
                    st.settle(dve)
                    st.by(V.tensor_scalar(t0, node, cand_f[:], None, ALU.is_lt))
                    st.settle(dve)
                    st.by(V.tensor_tensor(t0, t0, t1, ALU.mult))
                    st.settle(dve)
                    st.by(V.tensor_tensor(chosen, chosen, t0, ALU.add))
                    st.settle(dve)
                    st.by(V.tensor_tensor(H[:, :, 0:D], Y[:], bc(chosen, 2, [P, NT, D]), ALU.mult))
                    st.settle(dve)
                    dve.sem_inc(s_tile, 1)
            dve.sem_inc(s_last, 1)


_OUTS = [((6250, 128), "float32")]


def laid_out(inputs):
    arrays = {n: v for n, v in inputs.items() if n not in ("L1_gnn_queries",)}
    for new, old in (("W0T", "L0_gnn_W"), ("WfT", "L1_gnn_W_fwd"), ("WbT", "L1_gnn_W_back")):
        arrays[new] = arrays.pop(old).T
    return arrays


def kernel(**inputs):
    import numpy as _np
    import concourse.bacc as _bacc
    from concourse import mybir as _mybir
    from concourse.bass_utils import run_bass_kernel_spmd as _run

    nc = _bacc.Bacc("TRN2", target_bir_lowering=False, num_devices=1)
    arrays, args = {}, {}
    for name, v in laid_out(inputs).items():
        v = _np.ascontiguousarray(v)
        arrays[name] = v
        args[name] = nc.dram_tensor(name, v.shape, _mybir.dt.from_np(v.dtype), kind="ExternalInput").ap()
    (shape, dtype), = _OUTS
    out = nc.dram_tensor("out_x", shape, _mybir.dt.from_np(_np.dtype(dtype)), kind="ExternalOutput").ap()
    gnn_kernel(nc, args, out)
    r = _run(nc, [arrays], core_ids=[0])
    return r.results[0]["out_x"]
```
